# Optimizing a Trainium2 kernel written in Bass

```python
import numpy as np
import jax
import jax.numpy as jnp

def _softmax(x, axis=-1):
    return jax.nn.softmax(x, axis=axis)

def _gelu(x):
    return jax.nn.gelu(x, approximate=True)

def _silu(x):
    return jax.nn.silu(x)

def _sigmoid(x):
    return jax.nn.sigmoid(x)

def _layernorm(x, axis=-1, eps=1e-05):
    m = jnp.mean(x, axis=axis, keepdims=True)
    v = jnp.var(x, axis=axis, keepdims=True)
    return (x - m) / jnp.sqrt(v + eps)

def _scatter_add(tgt, idx, src, axis=0):
    return tgt.at[idx].add(src)

def _segment_sum(src, seg, n):
    return jax.ops.segment_sum(src, seg, n)
kernel_name = 'mk_perceiver_d2_seqx_r2_4e9af7'

def setup_inputs(seed: int=0):
    np.random.seed(seed)
    _w = jnp.asarray

    def _rec_inputs():
        import jax
        import jax.numpy as jnp
        _rk = jax.random.key(seed)
        x = -0.0005207 + 1.001 * jax.random.normal(jax.random.fold_in(_rk, 1), (2, 128, 512), jnp.float32)
        _lenS = 128 - jax.random.randint(jax.random.fold_in(_rk, 7), (2,), 0, max(1, 128 // 4) + 1, jnp.int32)
        _lenS2 = 2048 - jax.random.randint(jax.random.fold_in(_rk, 8), (2,), 0, max(1, 2048 // 4) + 1, jnp.int32)
        _ctx_1024P = jax.random.normal(jax.random.fold_in(_rk, 11), (2, 16, 512), jnp.float32)
        _ctx_1024c = jax.random.dirichlet(jax.random.fold_in(_rk, 511), 0.3 * jnp.ones((16,), jnp.float32), (2, 2048))
        _ctx_1024t = jnp.einsum('bsk,bkd->bsd', _ctx_1024c, _ctx_1024P)
        _ctx_1024t = _ctx_1024t * jax.lax.rsqrt(jnp.mean(jnp.square(_ctx_1024t)) + 1e-12) * 0.953939
        ctx_1024 = -1.52775e-05 + 0.999936 * (_ctx_1024t + 0.3 * jax.random.normal(jax.random.fold_in(_rk, 611), (2, 2048, 512), jnp.float32))
        _validS = jnp.arange(128)[None, :] < _lenS[:, None]
        _validS2 = jnp.arange(2048)[None, :] < _lenS2[:, None]
        _causal = jnp.tril(jnp.ones((128, 128), dtype=bool))
        mask_Bx1xSxS2_ff0 = jnp.where(jnp.ones((2, 1, 128, 2048), dtype=bool), 0.0, -1000000000.0).astype(jnp.float32)
        return (x, ctx_1024, mask_Bx1xSxS2_ff0)
    x, ctx_1024, mask_Bx1xSxS2_ff0 = _rec_inputs()

    def _L0_xattn_setup():
        import jax, jax.numpy as jnp
        import numpy as np
        DIM = 512
        HEADS = 16
        DHEAD = 64
        INNER = HEADS * DHEAD
        EPS = 1e-05

        def layer_norm(x, g, b):
            mu = jnp.mean(x, axis=-1, keepdims=True)
            var = jnp.mean(jnp.square(x - mu), axis=-1, keepdims=True)
            return (x - mu) * jax.lax.rsqrt(var + EPS) * g + b

        def apply_rope(x, cos, sin):
            d2 = x.shape[-1] // 2
            x1, x2 = (x[..., :d2], x[..., d2:])
            return jnp.concatenate([x1 * cos - x2 * sin, x2 * cos + x1 * sin], axis=-1)
        key = jax.random.key(seed)
        ks = jax.random.split(key, 10)
        B, N, S = (8, 128, 2048)
        latents = jax.random.normal(ks[0], (B, N, DIM), dtype=jnp.float32)
        context = jax.random.normal(ks[1], (B, S, DIM), dtype=jnp.float32)
        cos = jax.random.uniform(ks[2], (S, DHEAD // 2), dtype=jnp.float32)
        sin = jax.random.uniform(ks[3], (S, DHEAD // 2), dtype=jnp.float32)
        init = lambda k, shp, fan_in: jax.random.normal(k, shp, dtype=jnp.float32) / np.sqrt(fan_in)
        return {'latents': latents, 'context': context, 'cos': cos, 'sin': sin, 'ln_lat_g': jnp.ones((DIM,), jnp.float32), 'ln_lat_b': jnp.zeros((DIM,), jnp.float32), 'ln_ctx_g': jnp.ones((DIM,), jnp.float32), 'ln_ctx_b': jnp.zeros((DIM,), jnp.float32), 'Wq': init(ks[4], (DIM, INNER), DIM), 'Wkv': init(ks[5], (DIM, 2 * INNER), DIM), 'Wo': init(ks[6], (INNER, DIM), INNER), 'bo': jnp.zeros((DIM,), jnp.float32)}
    _L0_xattn_all = _L0_xattn_setup()
    _L0_xattn_in = {k: v for k, v in _L0_xattn_all.items() if k in ('cos', 'sin', 'ln_lat_g', 'ln_lat_b', 'ln_ctx_g', 'ln_ctx_b', 'Wq', 'Wkv', 'Wo', 'bo')}
    del _L0_xattn_all

    def _L0_attn_setup():
        import jax, jax.numpy as jnp
        import numpy as np
        N_HEAD = 16
        NEG_BIG = -10000000000.0

        def _rope_cos_sin(T, head_dim, dtype):
            half = head_dim // 2
            i = jnp.arange(half, dtype=jnp.float32)
            theta = 1.0 / 10000.0 ** (2.0 * i / head_dim)
            t = jnp.arange(T, dtype=jnp.float32)[:, None]
            ang = t * theta[None, :]
            return (jnp.cos(ang).astype(dtype), jnp.sin(ang).astype(dtype))

        def _apply_rope(x, cos, sin):
            B, H, T, D = x.shape
            xr = x.reshape(B, H, T, D // 2, 2)
            x0, x1 = (xr[..., 0], xr[..., 1])
            c = cos[None, None, :, :]
            s = sin[None, None, :, :]
            out = jnp.stack((x0 * c - x1 * s, x0 * s + x1 * c), axis=-1)
            return out.reshape(B, H, T, D)
        key = jax.random.key(seed)
        ks = jax.random.split(key, 9)
        B, T, C = (4, 1024, 512)
        sc = 1.0 / np.sqrt(C)
        return {'x': jax.random.normal(ks[0], (B, T, C), jnp.float32), 'wq': jax.random.normal(ks[1], (C, C), jnp.float32) * sc, 'bq': jax.random.normal(ks[2], (C,), jnp.float32) * 0.02, 'wk': jax.random.normal(ks[3], (C, C), jnp.float32) * sc, 'bk': jax.random.normal(ks[4], (C,), jnp.float32) * 0.02, 'wv': jax.random.normal(ks[5], (C, C), jnp.float32) * sc, 'bv': jax.random.normal(ks[6], (C,), jnp.float32) * 0.02, 'wp': jax.random.normal(ks[7], (C, C), jnp.float32) * sc, 'bp': jax.random.normal(ks[8], (C,), jnp.float32) * 0.02}
    _L0_attn_all = _L0_attn_setup()
    _L0_attn_in = {k: v for k, v in _L0_attn_all.items() if k in ('wq', 'bq', 'wk', 'bk', 'wv', 'bv', 'wp', 'bp')}
    del _L0_attn_all

    def _L0_ffn_setup():
        import jax, jax.numpy as jnp
        import numpy as np
        key = jax.random.key(seed)
        kx, kw = jax.random.split(key)
        x = jax.random.normal(kx, (32, 2048, 512), dtype=jnp.float32)
        weight = jax.random.normal(kw, (512, 512), dtype=jnp.float32) * 0.01
        return {'x': x, 'weight': weight}
    _L0_ffn_all = _L0_ffn_setup()
    _L0_ffn_in = {k: v for k, v in _L0_ffn_all.items() if k in ('weight',)}
    del _L0_ffn_all

    def _L1_xattn_setup():
        import jax, jax.numpy as jnp
        import numpy as np
        HIDDEN = 512
        HEADS = 16
        N, T1, T2 = (2, 1024, 1024)

        def _split_heads(x):
            n, t, e = x.shape
            return x.reshape(n, t, HEADS, e // HEADS).transpose(0, 2, 1, 3)
        key = jax.random.key(seed)
        k1, k2, k3, k4 = jax.random.split(key, 4)
        q = jax.random.normal(k1, (N, T1, HIDDEN), dtype=jnp.float32)
        encoder_k = jax.random.normal(k2, (N, T2, HIDDEN), dtype=jnp.float32)
        encoder_v = jax.random.normal(k3, (N, T2, HIDDEN), dtype=jnp.float32)
        encoder_attention_mask = jnp.zeros((N, 1, T2, T2), dtype=jnp.float32)
        wo_w = jax.random.normal(k4, (HIDDEN, HIDDEN), dtype=jnp.float32) * (1.0 / np.sqrt(HIDDEN))
        wo_b = jnp.zeros((HIDDEN,), dtype=jnp.float32)
        return {'q': q, 'encoder_k': encoder_k, 'encoder_v': encoder_v, 'encoder_attention_mask': encoder_attention_mask, 'wo_w': wo_w, 'wo_b': wo_b}
    _L1_xattn_all = _L1_xattn_setup()
    _L1_xattn_in = {k: v for k, v in _L1_xattn_all.items() if k in ('wo_w', 'wo_b')}
    del _L1_xattn_all

    def _L1_attn_setup():
        import jax, jax.numpy as jnp
        import numpy as np
        B, T, C = (2, 1024, 512)
        H, DK, OUT = (16, 64, 512)
        key = jax.random.key(seed)
        k1, k2, k3, k4, k5 = jax.random.split(key, 5)
        glorot_qkv = (2.0 / (C + H * DK)) ** 0.5
        glorot_o = (2.0 / (H * DK + OUT)) ** 0.5
        return {'x': jax.random.normal(k1, (B, T, C), dtype=jnp.float32), 'query_mat': jax.random.normal(k2, (C, H, DK), dtype=jnp.float32) * glorot_qkv, 'key_mat': jax.random.normal(k3, (C, H, DK), dtype=jnp.float32) * glorot_qkv, 'value_mat': jax.random.normal(k4, (C, H, DK), dtype=jnp.float32) * glorot_qkv, 'linear_m1': jax.random.normal(k5, (H * DK, OUT), dtype=jnp.float32) * glorot_o}
    _L1_attn_all = _L1_attn_setup()
    _L1_attn_in = {k: v for k, v in _L1_attn_all.items() if k in ('query_mat', 'key_mat', 'value_mat', 'linear_m1')}
    del _L1_attn_all

    def _L1_ffn_setup():
        import jax, jax.numpy as jnp
        import numpy as np
        E = 8
        K = 2
        D = 512
        P = 2048
        key = jax.random.key(seed)
        ks = jax.random.split(key, 8)
        s = lambda fan_in: 1.0 / np.sqrt(fan_in)
        x = jax.random.normal(ks[0], (2, 1024, D), dtype=jnp.float32)
        W1 = jax.random.normal(ks[1], (E, D, P), dtype=jnp.float32) * s(D)
        b1 = jax.random.normal(ks[2], (E, P), dtype=jnp.float32) * 0.01
        W2 = jax.random.normal(ks[3], (E, P, D), dtype=jnp.float32) * s(P)
        b2 = jax.random.normal(ks[4], (E, D), dtype=jnp.float32) * 0.01
        Wr = jax.random.normal(ks[5], (D, E), dtype=jnp.float32) * s(D)
        br = jax.random.normal(ks[6], (E,), dtype=jnp.float32) * 0.01
        return {'x': x, 'W1': W1, 'b1': b1, 'W2': W2, 'b2': b2, 'Wr': Wr, 'br': br}
    _L1_ffn_all = _L1_ffn_setup()
    _L1_ffn_in = {k: v for k, v in _L1_ffn_all.items() if k in ('W1', 'b1', 'W2', 'b2', 'Wr', 'br')}
    del _L1_ffn_all
    return {'x': x, 'ctx_1024': ctx_1024, 'mask_Bx1xSxS2_ff0': mask_Bx1xSxS2_ff0, 'L0_xattn_cos': _L0_xattn_in['cos'], 'L0_xattn_sin': _L0_xattn_in['sin'], 'L0_xattn_ln_lat_g': _L0_xattn_in['ln_lat_g'], 'L0_xattn_ln_lat_b': _L0_xattn_in['ln_lat_b'], 'L0_xattn_ln_ctx_g': _L0_xattn_in['ln_ctx_g'], 'L0_xattn_ln_ctx_b': _L0_xattn_in['ln_ctx_b'], 'L0_xattn_Wq': _L0_xattn_in['Wq'], 'L0_xattn_Wkv': _L0_xattn_in['Wkv'], 'L0_xattn_Wo': _L0_xattn_in['Wo'], 'L0_xattn_bo': _L0_xattn_in['bo'], 'L0_attn_wq': _L0_attn_in['wq'], 'L0_attn_bq': _L0_attn_in['bq'], 'L0_attn_wk': _L0_attn_in['wk'], 'L0_attn_bk': _L0_attn_in['bk'], 'L0_attn_wv': _L0_attn_in['wv'], 'L0_attn_bv': _L0_attn_in['bv'], 'L0_attn_wp': _L0_attn_in['wp'], 'L0_attn_bp': _L0_attn_in['bp'], 'L0_ffn_weight': _L0_ffn_in['weight'], 'L1_xattn_wo_w': _L1_xattn_in['wo_w'], 'L1_xattn_wo_b': _L1_xattn_in['wo_b'], 'L1_attn_query_mat': _L1_attn_in['query_mat'], 'L1_attn_key_mat': _L1_attn_in['key_mat'], 'L1_attn_value_mat': _L1_attn_in['value_mat'], 'L1_attn_linear_m1': _L1_attn_in['linear_m1'], 'L1_ffn_W1': _L1_ffn_in['W1'], 'L1_ffn_b1': _L1_ffn_in['b1'], 'L1_ffn_W2': _L1_ffn_in['W2'], 'L1_ffn_b2': _L1_ffn_in['b2'], 'L1_ffn_Wr': _L1_ffn_in['Wr'], 'L1_ffn_br': _L1_ffn_in['br']}

def reference(x, ctx_1024, mask_Bx1xSxS2_ff0, L0_xattn_cos, L0_xattn_sin, L0_xattn_ln_lat_g, L0_xattn_ln_lat_b, L0_xattn_ln_ctx_g, L0_xattn_ln_ctx_b, L0_xattn_Wq, L0_xattn_Wkv, L0_xattn_Wo, L0_xattn_bo, L0_attn_wq, L0_attn_bq, L0_attn_wk, L0_attn_bk, L0_attn_wv, L0_attn_bv, L0_attn_wp, L0_attn_bp, L0_ffn_weight, L1_xattn_wo_w, L1_xattn_wo_b, L1_attn_query_mat, L1_attn_key_mat, L1_attn_value_mat, L1_attn_linear_m1, L1_ffn_W1, L1_ffn_b1, L1_ffn_W2, L1_ffn_b2, L1_ffn_Wr, L1_ffn_br):
    import jax
    import jax.numpy as jnp

    def _L0_xattn_ref(latents, context, cos, sin, ln_lat_g, ln_lat_b, ln_ctx_g, ln_ctx_b, Wq, Wkv, Wo, bo):
        import jax, jax.numpy as jnp
        import numpy as np
        DIM = 512
        HEADS = 16
        DHEAD = 64
        INNER = HEADS * DHEAD
        EPS = 1e-05

        def layer_norm(x, g, b):
            mu = jnp.mean(x, axis=-1, keepdims=True)
            var = jnp.mean(jnp.square(x - mu), axis=-1, keepdims=True)
            return (x - mu) * jax.lax.rsqrt(var + EPS) * g + b

        def apply_rope(x, cos, sin):
            d2 = x.shape[-1] // 2
            x1, x2 = (x[..., :d2], x[..., d2:])
            return jnp.concatenate([x1 * cos - x2 * sin, x2 * cos + x1 * sin], axis=-1)
        b, n, _ = latents.shape
        s = context.shape[1]
        lat = layer_norm(latents, ln_lat_g, ln_lat_b)
        ctx = layer_norm(context, ln_ctx_g, ln_ctx_b)
        q = (lat @ Wq).reshape(b, n, HEADS, DHEAD).transpose(0, 2, 1, 3)
        kv = ctx @ Wkv
        k, v = jnp.split(kv, 2, axis=-1)
        k = k.reshape(b, s, HEADS, DHEAD).transpose(0, 2, 1, 3)
        v = v.reshape(b, s, HEADS, DHEAD).transpose(0, 2, 1, 3)
        k = apply_rope(k, cos[None, None], sin[None, None])
        scale = DHEAD ** (-0.5)
        attn = jnp.einsum('bhnd,bhsd->bhns', q, k) * scale
        attn = jnp.clip(attn, -11.0, 11.0)
        attn = jax.nn.softmax(attn, axis=-1)
        out = jnp.einsum('bhns,bhsd->bhnd', attn, v)
        out = out.transpose(0, 2, 1, 3).reshape(b, n, INNER)
        return out @ Wo + bo

    def _L0_attn_ref(x, wq, bq, wk, bk, wv, bv, wp, bp):
        import jax, jax.numpy as jnp
        import numpy as np
        N_HEAD = 16
        NEG_BIG = -10000000000.0

        def _rope_cos_sin(T, head_dim, dtype):
            half = head_dim // 2
            i = jnp.arange(half, dtype=jnp.float32)
            theta = 1.0 / 10000.0 ** (2.0 * i / head_dim)
            t = jnp.arange(T, dtype=jnp.float32)[:, None]
            ang = t * theta[None, :]
            return (jnp.cos(ang).astype(dtype), jnp.sin(ang).astype(dtype))

        def _apply_rope(x, cos, sin):
            B, H, T, D = x.shape
            xr = x.reshape(B, H, T, D // 2, 2)
            x0, x1 = (xr[..., 0], xr[..., 1])
            c = cos[None, None, :, :]
            s = sin[None, None, :, :]
            out = jnp.stack((x0 * c - x1 * s, x0 * s + x1 * c), axis=-1)
            return out.reshape(B, H, T, D)
        B, T, C = x.shape
        H = N_HEAD
        D = C // H

        def proj(w, b):
            return (jnp.einsum('btc,oc->bto', x, w) + b).reshape(B, T, H, D).transpose(0, 2, 1, 3)
        q = proj(wq, bq)
        k = proj(wk, bk)
        v = proj(wv, bv)
        cos, sin = _rope_cos_sin(T, D, x.dtype)
        q = _apply_rope(q, cos, sin)
        k = _apply_rope(k, cos, sin)
        att = jnp.einsum('bhtd,bhsd->bhts', q, k) * (1.0 / np.sqrt(D))
        causal = jnp.tril(jnp.ones((T, T), bool))
        att = jnp.where(causal[None, None], att, jnp.asarray(NEG_BIG, att.dtype))
        att = jax.nn.softmax(att, axis=-1)
        y = jnp.einsum('bhts,bhsd->bhtd', att, v)
        y = y.transpose(0, 2, 1, 3).reshape(B, T, C)
        return jnp.einsum('btc,oc->bto', y, wp) + bp

    def _L0_ffn_ref(x, weight):
        import jax, jax.numpy as jnp
        import numpy as np
        b_weight = jnp.sign(weight)
        return jnp.einsum('bsi,oi->bso', x, b_weight)

    def _L1_xattn_ref(q, encoder_k, encoder_v, encoder_attention_mask, wo_w, wo_b):
        import jax, jax.numpy as jnp
        import numpy as np
        HIDDEN = 512
        HEADS = 16
        N, T1, T2 = (2, 1024, 1024)

        def _split_heads(x):
            n, t, e = x.shape
            return x.reshape(n, t, HEADS, e // HEADS).transpose(0, 2, 1, 3)
        qh = _split_heads(q)
        kh = _split_heads(encoder_k)
        vh = _split_heads(encoder_v)
        scores = jnp.einsum('bhqd,bhkd->bhqk', qh, kh) + encoder_attention_mask
        weights = jax.nn.softmax(scores, axis=-1)
        ctx = jnp.einsum('bhqk,bhkd->bhqd', weights, vh)
        ctx = ctx.transpose(0, 2, 1, 3).reshape(q.shape[0], q.shape[1], -1)
        return jax.nn.relu(ctx @ wo_w.T + wo_b)

    def _L1_attn_ref(x, query_mat, key_mat, value_mat, linear_m1):
        import jax, jax.numpy as jnp
        import numpy as np
        B, T, C = (2, 1024, 512)
        H, DK, OUT = (16, 64, 512)
        q = jnp.einsum('btc,chd->bhtd', x, query_mat)
        k = jnp.einsum('btc,chd->bhtd', x, key_mat)
        v = jnp.einsum('btc,chd->bhtd', x, value_mat)
        d_k = query_mat.shape[-1]
        w = jnp.einsum('bhtd,bhzd->bhtz', q, k) * d_k ** 0.5
        t = w.shape[-1]
        causal = jnp.tril(jnp.ones((t, t), dtype=bool))
        w = jnp.where(causal, w, -jnp.inf)
        w = jax.nn.softmax(w, axis=-1)
        o = jnp.einsum('bhtz,bhzd->bhtd', w, v)
        o = o.transpose(0, 2, 1, 3).reshape(o.shape[0], o.shape[2], -1)
        return jnp.einsum('btc,cz->btz', o, linear_m1)

    def _L1_ffn_ref(x, W1, b1, W2, b2, Wr, br):
        import jax, jax.numpy as jnp
        import numpy as np
        E = 8
        K = 2
        D = 512
        P = 2048
        B, S, _ = x.shape
        xf = x.reshape(B * S, D)
        scores = xf @ Wr + br
        _, top_idx = jax.lax.top_k(scores, K)
        mask = jax.nn.one_hot(top_idx, E, dtype=scores.dtype).sum(-2) > 0
        router_weights = jax.nn.softmax(jnp.where(mask, scores, -jnp.inf), axis=-1)
        h = jax.nn.gelu(jnp.einsum('td,edp->etp', xf, W1) + b1[:, None, :])
        y = jnp.einsum('etp,epd->etd', h, W2) + b2[:, None, :]
        out = jnp.einsum('te,etd->td', router_weights, y)
        return out.reshape(B, S, D)
    x = x + _L0_xattn_ref(_layernorm(x, axis=-1), ctx_1024, L0_xattn_cos, L0_xattn_sin, L0_xattn_ln_lat_g, L0_xattn_ln_lat_b, L0_xattn_ln_ctx_g, L0_xattn_ln_ctx_b, L0_xattn_Wq, L0_xattn_Wkv, L0_xattn_Wo, L0_xattn_bo)
    x = x + _L0_attn_ref(_layernorm(x, axis=-1), L0_attn_wq, L0_attn_bq, L0_attn_wk, L0_attn_bk, L0_attn_wv, L0_attn_bv, L0_attn_wp, L0_attn_bp)
    x = x + _L0_ffn_ref(_layernorm(x, axis=-1), L0_ffn_weight)
    x = x + _L1_xattn_ref(_layernorm(x, axis=-1), ctx_1024, ctx_1024, mask_Bx1xSxS2_ff0, L1_xattn_wo_w, L1_xattn_wo_b)
    x = x + _L1_attn_ref(_layernorm(x, axis=-1), L1_attn_query_mat, L1_attn_key_mat, L1_attn_value_mat, L1_attn_linear_m1)
    x = x + _L1_ffn_ref(_layernorm(x, axis=-1), L1_ffn_W1, L1_ffn_b1, L1_ffn_W2, L1_ffn_b2, L1_ffn_Wr, L1_ffn_br)
    return x

_drawn_inputs = setup_inputs


def setup_inputs(seed=0):
    import zlib

    import numpy as np

    out = dict(_drawn_inputs(seed))
    spreads = {'L0_xattn_ln_lat_g': (1.0, 0.6),
     'L0_xattn_ln_lat_b': (0.0, 0.605),
     'L0_xattn_ln_ctx_g': (1.0, 0.2),
     'L0_xattn_ln_ctx_b': (0.0, 0.1),
     'L0_xattn_bo': (0.0, 0.1),
     'L1_xattn_wo_b': (0.0, 2.0)}
    factors = {'L0_xattn_cos': 8.0,
     'L0_xattn_sin': 8.0,
     'L0_attn_bq': 8.0,
     'L0_attn_bk': 21.929,
     'L0_attn_bv': 3.945,
     'L0_attn_bp': 4.372,
     'L1_ffn_W1': 3.421,
     'L1_ffn_b1': 64.0,
     'L1_ffn_W2': 3.072,
     'L1_ffn_b2': 176.856,
     'L1_ffn_Wr': 3.473,
     'L1_ffn_br': 35.348}
    for name, (base, spread) in spreads.items():
        noise = np.random.default_rng([zlib.crc32(name.encode()), seed]).standard_normal(out[name].shape)
        drawn = base * np.exp(spread * noise) if base else spread * noise
        out[name] = jnp.asarray(drawn.astype(out[name].dtype))
    for name, factor in factors.items():
        out[name] = (out[name] * factor).astype(out[name].dtype)
    return out
```

```python
from contextlib import ExitStack

import concourse.bass as bass
from concourse import mybir

F32 = mybir.dt.float32
F32R = mybir.dt.float32r
ACT = mybir.ActivationFunctionType
ALU = mybir.AluOpType
AX = mybir.AxisListType

P = 128
NB = 2
D = 512
KD = D // P
S = 2048
NCH = S // P
NG = S // 512
TOK = NB * P
EPS = 1e-5

H = 16
DH0 = 64
DHS = 32
NQ = 4
E_MOE = 8
F_MOE = 2048
NU = F_MOE // 512
MASKED = -1e30

LO_CLIP = 1.670170079024566e-05
HI_CLIP = 59874.14171519782


class Chain:

    def __init__(self, eng, sem, start=0):
        self.eng, self.sem, self.n = eng, sem, start

    def __call__(self, ins):
        self.n += 1
        ins.then_inc(self.sem, 1)
        self.eng.wait_ge(self.sem, self.n)


def split_matmul(pe, out, w_hi, w_lo, x_hi, x_lo, start, stop):
    pe.matmul(out, w_hi, x_hi, start=start, stop=False)
    pe.matmul(out, w_hi, x_lo, start=False, stop=False)
    return pe.matmul(out, w_lo, x_hi, start=False, stop=stop)


def program(nc, I, out):
    top = ExitStack()
    with top:
        def sem(name):
            return top.enter_context(nc.semaphore(name))

        def sb_in(stack, name, shape, dt=F32):
            return stack.enter_context(nc.sbuf_tensor(name, shape, dt))

        def ps_in(stack, name, shape):
            return stack.enter_context(nc.psum_tensor(name, shape, F32))

        resid = sb_in(top, "resid", [P, NB, D])
        ident = sb_in(top, "ident", [P, P])
        ones_row = sb_in(top, "ones_row", [1, P])
        normed = sb_in(top, "normed", [P, NB, D])
        normed_T = sb_in(top, "normed_T", [P, KD, TOK])
        ln_stats = sb_in(top, "ln_stats", [P, NB, 6])
        ln_mv = sb_in(top, "ln_mv", [P, NB, 2])
        ln_var = sb_in(top, "ln_var", [P, NB])
        ln_std = sb_in(top, "ln_std", [P, NB])
        ln_rstd = sb_in(top, "ln_rstd", [P, NB])

        consts_in = sem("consts_in")
        ones_set = sem("ones_set")

        dve_step, var_ready, std_ready, ln_ready, T_ready, T_done = (
            sem(f"ln_{n}") for n in ("dve_step", "var_ready", "std_ready", "ln_ready", "T_ready", "T_done"))
        ln_count = {"step": 0, "var": 0, "ln": 0, "T": 0}

        def layer_norm_T(tag, times=1, scale_bias=None, first_wait=None):
            step0, var0, ln0, T0 = (ln_count[n] for n in ("step", "var", "ln", "T"))
            ln_count["step"] += 7 * times - 2 if times > 1 else 5
            ln_count["var"] += times
            ln_count["ln"] += NB
            ln_count["T"] += 2
            with ExitStack() as st:
                T_ps = ps_in(st, f"{tag}_T_ps", [P, KD, TOK])
                block = st.enter_context(nc.Block())

                @block.vector
                def _(dve):
                    if first_wait:
                        dve.wait_ge(*first_wait)
                    step = Chain(dve, dve_step, step0)
                    for t in range(times):
                        src = resid if t == 0 else normed
                        for b in range(NB):
                            step(dve.bn_stats(ln_stats[:, b, :], src[:, b, :]))
                        for b in range(NB):
                            step(dve.bn_aggr(ln_mv[:, b, :], ln_stats[:, b, :]))
                        dve.tensor_scalar(ln_var[:], ln_mv[:, :, 1], EPS, None, ALU.add).then_inc(var_ready, 1)
                        dve.wait_ge(std_ready, var0 + t + 1)
                        step(dve.reciprocal(ln_rstd[:], ln_std[:]))
                        for b in range(NB):
                            ins = dve.tensor_scalar(normed[:, b, :], src[:, b, :], ln_mv[:, b, 0:1],
                                                    ln_rstd[:, b:b + 1], ALU.subtract, ALU.mult)
                            if t < times - 1:
                                step(ins)
                            else:
                                ins.then_inc(ln_ready, 1)

                @block.scalar
                def _(act):
                    for t in range(times):
                        act.wait_ge(var_ready, var0 + t + 1)
                        act.activation(ln_std[:], ln_var[:], ACT.Sqrt).then_inc(std_ready, 1)
                    if scale_bias is None:
                        for half in range(2):
                            act.wait_ge(T_ready, T0 + half + 1)
                            act.activation(normed_T[:, 2 * half:2 * half + 2, :], T_ps[:, 2 * half:2 * half + 2, :],
                                           ACT.Copy).then_inc(T_done, 1)
                    else:
                        g_col, b_col = scale_bias
                        for k in range(KD):
                            act.wait_ge(T_ready, T0 + k // 2 + 1)
                            act.activation(normed_T[:, k, :], T_ps[:, k, :], ACT.Identity,
                                           bias=b_col[:, k:k + 1], scale=g_col[:, k:k + 1]).then_inc(T_done, 1)

                @block.tensor
                def _(pe):
                    pe.wait_ge(ln_ready, ln0 + NB)
                    if first_wait:
                        pe.wait_ge(*first_wait)
                    for k in range(KD):
                        for b in range(NB):
                            ins = pe.transpose(T_ps[:, k, b * P:(b + 1) * P], normed[:, b, k * P:(k + 1) * P],
                                               ident[:])
                        if k % 2:
                            ins.then_inc(T_ready, 1)

        with nc.Block() as block:
            @block.sync
            def _(sp):
                for b in range(NB):
                    sp.dma_start(resid[:, b, :], I["x"][b]).then_inc(consts_in, 16)
                sp.dma_start(ident[:], I["ident"]).then_inc(consts_in, 16)

            @block.vector
            def _(dve):
                dve.memset(ones_row[:], 1.0).then_inc(ones_set, 1)

        cross_attention_rotary(nc, I, locals())
        with ExitStack() as after:
            behind_cross_attention(nc, I, locals(), after)

        stored = sem("stored")
        with nc.Block() as block:
            @block.sync
            def _(sp):
                for b in range(NB):
                    sp.dma_start(out[b], resid[:, b, :]).then_inc(stored, 16)
                sp.wait_ge(stored, 16 * NB)


def behind_cross_attention(nc, I, env, outer):
    sem, sb_in = env["sem"], env["sb_in"]

    def load_block(name, loads):
        got = sem(name)
        with nc.Block() as block:
            @block.sync
            def _(sp):
                for dst, src in loads:
                    sp.dma_start(dst, src).then_inc(got, 16)
        return got

    rows4 = lambda n: I[n].rearrange("(k p) n -> p k n", p=P)
    env["sa1_w"] = [sb_in(outer, f"sa1_{n}", [P, KD, 1024]) for n in ("wq", "wk", "wv")]
    env["sa1_wq"], env["sa1_wk"], env["sa1_wv"] = env["sa1_w"]
    causal = sb_in(outer, "causal", [P, D])
    env["sa0_mask"] = env["sa1_mask"] = causal
    env["sa1_rows"] = env["sa1_rc"] = env["sa1_rs"] = None
    with ExitStack() as st:
        loads = [(causal[:], I["causal4"])]
        for n in ("wq", "wk", "wv", "wp"):
            env["sa0_" + n] = sb_in(st, "sa0_" + n, [P, KD, D])
        env["sa0_rows"] = sb_in(st, "sa0_rows", [1, 4 * D])
        for n in ("rc", "rs"):
            env["sa0_" + n] = sb_in(st, "sa0_" + n, [P, D])
        sgn_w = sb_in(st, "sgn_w", [P, KD, D])
        loads += [(env["sa0_" + n][:], rows4("sa0_" + n)) for n in ("wq", "wk", "wv")]
        loads += [(env["sa0_rows"][:], I["sa0_rows"]), (env["sa0_rc"][:], I["sa0_rc"]),
                  (env["sa0_rs"][:], I["sa0_rs"]), (env["sa0_wp"][:], rows4("sa0_wp"))]
        env["sa0_w_in"], env["sa0_w_count"] = load_block("sa0_w_in", loads), len(loads)
        env["sgn_w"], env["sgn_w_need"] = sgn_w, 16
        env["sgn_w_in"] = load_block("sgn_w_in", [(sgn_w[:], rows4("sgn_w"))])
        self_attention(nc, I, env, "sa0", DHS, 0)
        if STOP >= 3:
            sign_layer(nc, I, env)
    if STOP >= 4:
        with ExitStack() as st:
            env["wo1"] = sb_in(st, "wo1", [P, KD, D])
            env["wo1_row"] = sb_in(st, "wo1_row", [1, D])
            env["wo1_in"] = load_block("wo1_in", [(env["wo1"][:], rows4("wo1")), (env["wo1_row"][:], I["wo1_row"])])
            env["wo1_need"] = 32
            cross_attention_masked(nc, I, env)
    if STOP >= 5:
        with ExitStack() as st:
            wp = env["sa1_wp"] = sb_in(st, "sa1_wp", [P, 8, D])
            loads = [(t[:], rows4(n)) for t, n in zip(env["sa1_w"], ("sa1_wq", "sa1_wk", "sa1_wv"))]
            loads += [(wp[:], rows4("sa1_wp"))]
            env["sa1_w_in"], env["sa1_w_count"] = load_block("sa1_w_in", loads), len(loads)
            self_attention(nc, I, env, "sa1", DH0, 1)
    outer.close()
    if STOP >= 6:
        with ExitStack() as st:
            env["w1_raw"] = sb_in(st, "w1_raw", [P, 2, KD, 512])
            env["w2_raw"] = sb_in(st, "w2_raw", [P, 2, 4, D])
            env["w1_in"], env["w2_in"] = ([sem(f"{n}_in{r}") for r in range(2)] for n in ("w1", "w2"))
            with nc.Block() as block:
                @block.sync
                def _(sp):
                    for U in range(2):
                        for raw, name, got in ((env["w1_raw"], "w1", env["w1_in"]), (env["w2_raw"], "w2", env["w2_in"])):
                            sp.dma_start(raw[:, U, :, :], I[name][U * P:(U + 1) * P, :]
                                         .rearrange("p (k n) -> p k n", k=4)).then_inc(got[U], 16)
            experts(nc, I, env)


def cross_attention_rotary(nc, I, env):
    sem, sb_in, ps_in = env["sem"], env["sb_in"], env["ps_in"]
    resid, ident, ones_row, normed_T = env["resid"], env["ident"], env["ones_row"], env["normed_T"]
    consts_in = env["consts_in"]

    outer = ExitStack()
    with outer:
        q_stack = sb_in(outer, "q_stack", [P, NB * H * P])
        attn = sb_in(outer, "attn", [P, NB * H * DH0])
        vecs = sb_in(outer, "vecs", [P, 4 * KD + 1])
        lat_g, lat_b = vecs[:, 0:KD], vecs[:, KD:2 * KD]
        ctx_g, ctx_b = vecs[:, 2 * KD:3 * KD], vecs[:, 3 * KD:4 * KD]
        q_sign = vecs[:, 4 * KD:4 * KD + 1]

        wq_in, q_ready, q_done, vecs_in = (sem(n) for n in ("wq_in", "q_ready", "q_done", "vecs_in"))
        with ExitStack() as st:
            wq = sb_in(st, "wq_stack", [P, KD, H * P])
            with nc.Block() as block:
                @block.sync
                def _(sp):
                    sp.dma_start(vecs[:], I["vecs"]).then_inc(vecs_in, 16)
                    for k in range(KD):
                        sp.dma_start(wq[:, k, :], I["wq_stack"][k * P:(k + 1) * P, :]).then_inc(wq_in, 16)

                @block.scalar
                def _(act):
                    act.wait_ge(vecs_in, 16)
            env["layer_norm_T"]("ln0", times=2, scale_bias=(lat_g, lat_b), first_wait=(consts_in, 48))
            q_ps = ps_in(st, "q_ps", [P, 4, 2, TOK])
            block = st.enter_context(nc.Block())

            @block.tensor
            def _(pe):
                pe.wait_ge(wq_in, 16 * KD)
                for h in range(H):
                    n = h // 2
                    if h % 2 == 0 and n >= 4:
                        pe.wait_ge(q_done, n - 3)
                    for k in range(KD):
                        ins = pe.matmul(q_ps[:, n % 4, h % 2, :], wq[:, k, h * P:(h + 1) * P], normed_T[:, k, :],
                                        start=(k == 0), stop=(k == KD - 1))
                    if h % 2:
                        ins.then_inc(q_ready, 1)

            @block.scalar
            def _(act):
                q_view = q_stack[:].rearrange("p (b h t) -> p h b t", b=NB, h=H)
                for n in range(H // 2):
                    act.wait_ge(q_ready, n + 1)
                    act.activation(q_view[:, 2 * n:2 * n + 2, :, :],
                                   q_ps[:, n % 4, :, :].rearrange("p h (b t) -> p h b t", b=NB), ACT.Copy,
                                   scale=q_sign).then_inc(q_done, 1)

        names = ("tab_in", "ctx_in0", "ctx_in1", "ctx_free", "cvar", "cstd", "ctp", "cfull", "csplit",
                 "cstep", "wv_in", "wk_in", "wk_hi_done", "wk_lo_done", "wv_hi_done", "wv_lo_done",
                 "v_mm", "v_out", "k_mm", "rope_done", "sc_done", "exp_done", "clip_done", "pv_done",
                 "norm_done", "qcur_done", "vones", "den_step", "norm_step")
        s = {n: sem("x0_" + n) for n in names}
        with ExitStack() as st:
            cos_T = sb_in(st, "cos_T", [P, S])
            sin_T = sb_in(st, "sin_T", [P, S])
            ctx_hi = sb_in(st, "ctx_hi", [P, KD, S], F32R)
            ctx_lo = sb_in(st, "ctx_lo", [P, KD, S], F32R)
            ctx_raw = sb_in(st, "ctx_raw", [P, 2, 4, D])
            cst = sb_in(st, "cst", [P, 2, 4, 6])
            cmv = sb_in(st, "cmv", [P, 2, 4, 2])
            cva = sb_in(st, "cva", [P, 2, 4])
            csd = sb_in(st, "csd", [P, 2, 4])
            crs = sb_in(st, "crs", [P, 2, 4])
            wv_raw = sb_in(st, "wv_raw", [P, KD, 256])
            wv_hi = sb_in(st, "wv_hi", [P, KD, 256], F32R)
            wv_lo = sb_in(st, "wv_lo", [P, KD, 256], F32R)
            wk_raw = sb_in(st, "wk_raw", [P, KD, 256])
            wk_hi = sb_in(st, "wk_hi", [P, KD, 256], F32R)
            wk_lo = sb_in(st, "wk_lo", [P, KD, 256], F32R)
            vals = sb_in(st, "vals", [P, NCH, 4, DH0 + 1])
            keys = sb_in(st, "keys", [P, 3, 2, 512])
            prob = sb_in(st, "prob", [P, 3, 2, 512])
            ctx_full = prob[:, 0:2, :, :].rearrange("p a b n -> p (a b) n")
            q_cur = sb_in(st, "q_cur", [P, 4 * P])
            rden = sb_in(st, "rden", [P, 4])
            k_ps = ps_in(st, "k_ps", [P, 2, 512])
            u_ps = ps_in(st, "u_ps", [P, 4, 512])
            o_ps = ps_in(st, "o_ps", [P, 2, 512])
            block = st.enter_context(nc.Block())

            @block.sync
            def _(sp):
                sp.dma_start(wv_raw[:], I["wv_quads"][0].rearrange("p (k n) -> p k n", k=KD)).then_inc(s["wv_in"], 16)
                for b in range(NB):
                    for grp in range(NG):
                        sp.wait_ge(s["ctx_free"], b * NG + (grp + 1))
                        sp.dma_start(ctx_raw[:, grp % 2, :, :],
                                     I["ctx_rows"][b * S + grp * 512:b * S + (grp + 1) * 512, :]
                                     .rearrange("(c p) d -> p c d", p=P)).then_inc(s[f"ctx_in{grp % 2}"], 16)
                    with sp.Fori(0, NQ) as g:
                        u = b * NQ + g
                        sp.wait_ge(s["wk_lo_done"], u + 1)
                        sp.dma_start(wk_raw[:], I["wk_rows"][bass.ds(g * P, P), :]
                                     .rearrange("p (k n) -> p k n", k=KD)).then_inc(s["wk_in"], 16)
                        sp.wait_ge(s["wv_lo_done"], u + 1)
                        sp.dma_start(wv_raw[:], I["wv_rows"][bass.ds(g * P + P, P), :]
                                     .rearrange("p (k n) -> p k n", k=KD)).then_inc(s["wv_in"], 16)

            @block.gpsimd
            def _(pool):
                pool.dma_start(cos_T[:], I["cos_T4"]).then_inc(s["tab_in"], 16)
                pool.dma_start(sin_T[:], I["sin_T4"]).then_inc(s["tab_in"], 16)
                pool.memset(vals[:, :, :, DH0:DH0 + 1], 1.0).then_inc(s["vones"], 1)

            @block.vector
            def _(dve):
                dve.sem_inc(s["ctx_free"], 2)
                dve.sem_inc(s["wk_lo_done"], 1)
                dve.wait_ge(s["wv_hi_done"], 1)
                dve.tensor_tensor(wv_lo[:], wv_raw[:], wv_hi[:], ALU.subtract).then_inc(s["wv_lo_done"], 1)
                dve.wait_ge(s["tab_in"], 32)
                for b in range(NB):
                    def center(grp):
                        r = grp % 2
                        base = b * 52 + grp * 13

                        def step(n, ins):
                            ins.then_inc(s["cstep"], 1)
                            dve.wait_ge(s["cstep"], base + n)
                        dve.wait_ge(s[f"ctx_in{r}"], b * 32 + 16 * (grp // 2 + 1))
                        for c in range(4):
                            dve.bn_stats(cst[:, r, c, :], ctx_raw[:, r, c, :]).then_inc(s["cstep"], 1)
                        dve.wait_ge(s["cstep"], base + 4)
                        for c in range(4):
                            ins = dve.bn_aggr(cmv[:, r, c, :], cst[:, r, c, :]).then_inc(s["cstep"], 1)
                        dve.wait_ge(s["cstep"], base + 8)
                        dve.tensor_scalar(cva[:, r, :], cmv[:, r, :, 1], EPS, None, ALU.add).then_inc(s["cvar"], 1)
                        dve.wait_ge(s["cstd"], b * NG + (grp + 1))
                        step(9, dve.reciprocal(crs[:, r, :], csd[:, r, :]))
                        for c in range(4):
                            ins = dve.tensor_scalar(ctx_raw[:, r, c, :], ctx_raw[:, r, c, :], cmv[:, r, c, 0:1],
                                                    crs[:, r, c:c + 1], ALU.subtract, ALU.mult)
                            ins.then_inc(s["cstep"], 1)

                    def split(grp):
                        for k in range(KD):
                            n = grp * KD + k
                            dve.wait_ge(s["cfull"], b * 16 + (n + 1))
                            dve.tensor_copy(ctx_hi[:, k, grp * 512:(grp + 1) * 512],
                                            ctx_full[:, k, :]).then_inc(s["csplit"], 1)
                            dve.wait_ge(s["csplit"], b * 32 + (2 * n + 1))
                            dve.tensor_tensor(ctx_lo[:, k, grp * 512:(grp + 1) * 512], ctx_full[:, k, :],
                                              ctx_hi[:, k, grp * 512:(grp + 1) * 512],
                                              ALU.subtract).then_inc(s["csplit"], 1)
                    center(0)
                    for grp in range(NG):
                        if grp + 1 < NG:
                            center(grp + 1)
                        split(grp)

                    with dve.Fori(0, NQ) as g:
                        u = b * NQ + g
                        dve.wait_ge(s["sc_done"], u * 16 + 1)
                        dve.tensor_copy(q_cur[:], q_stack[:, bass.ds(u * (4 * P), 4 * P)]).then_inc(s["qcur_done"], 1)
                        dve.wait_ge(s["wk_hi_done"], u + 1)
                        dve.tensor_tensor(wk_lo[:], wk_raw[:], wk_hi[:], ALU.subtract).then_inc(s["wk_lo_done"], 1)

                        def rope(n):
                            c = n % 4
                            dve.wait_ge(s["k_mm"], u * 8 + (n + 2))
                            if n >= 3:
                                dve.wait_ge(s["sc_done"], u * 16 + (2 * (n - 2) + 1))
                            for hh in range(2):
                                rows = slice(hh * 64, hh * 64 + 64)
                                for t, tab in enumerate((cos_T, sin_T)):
                                    dve.tensor_tensor(keys[64 * t:64 * t + 64, n % 3, hh, :], k_ps[rows, n % 2, :],
                                                      tab[rows, c * 512:(c + 1) * 512],
                                                      ALU.mult).then_inc(s["rope_done"], 1)

                        def clip(n):
                            for hh in range(2):
                                dve.wait_ge(s["exp_done"], u * 16 + (2 * n + hh + 1))
                                dve.tensor_scalar(prob[:, n % 3, hh, :], prob[:, n % 3, hh, :], LO_CLIP, HI_CLIP,
                                                  ALU.max, ALU.min).then_inc(s["clip_done"], 1)

                        def normalise(pr):
                            for hh in range(2):
                                i = 2 * pr + hh
                                dve.wait_ge(s["pv_done"], u * 16 + (2 * (4 * pr + 3) + hh + 2))
                                dve.reciprocal(rden[:, i:i + 1], o_ps[:, hh, DH0:DH0 + 1]).then_inc(s["den_step"], 1)
                                dve.wait_ge(s["den_step"], u * 4 + (i + 1))
                                dve.tensor_scalar(attn[:, bass.ds(u * (4 * DH0) + i * DH0, DH0)],
                                                  o_ps[:, hh, 0:DH0], rden[:, i:i + 1], None,
                                                  ALU.mult).then_inc(s["norm_done"], 1)
                        for n in range(8):
                            if n == 6:
                                normalise(0)
                            rope(n)
                            if n >= 1:
                                clip(n - 1)
                            if n == 4:
                                dve.wait_ge(s["wv_hi_done"], u + 2)
                                dve.tensor_tensor(wv_lo[:], wv_raw[:], wv_hi[:],
                                                  ALU.subtract).then_inc(s["wv_lo_done"], 1)
                        clip(7)
                        normalise(1)

            @block.scalar
            def _(act):
                act.wait_ge(s["wv_in"], 16)
                act.activation(wv_hi[:], wv_raw[:], ACT.Copy).then_inc(s["wv_hi_done"], 1)
                for b in range(NB):
                    def root(grp):
                        act.wait_ge(s["cvar"], b * NG + (grp + 1))
                        act.activation(csd[:, grp % 2, :], cva[:, grp % 2, :], ACT.Sqrt).then_inc(s["cstd"], 1)

                    root(0)
                    for grp in range(NG):
                        if grp + 1 < NG:
                            root(grp + 1)
                        for k in range(KD):
                            n = grp * KD + k
                            act.wait_ge(s["ctp"], b * 16 + (n + 1))
                            act.wait_ge(s["csplit"], b * 32 + max(2 * (n - 3), 1)) if n >= 4 else None
                            act.activation(ctx_full[:, k, :], u_ps[:, k, :], ACT.Identity, bias=ctx_b[:, k:k + 1],
                                           scale=ctx_g[:, k:k + 1]).then_inc(s["cfull"], 1)
                    with act.Fori(0, NQ) as g:
                        u = b * NQ + g
                        act.wait_ge(s["wk_in"], u * 16 + 16)
                        act.wait_ge(s["k_mm"], u * 8 + 1)
                        act.activation(wk_hi[:], wk_raw[:], ACT.Copy).then_inc(s["wk_hi_done"], 1)
                        for i in range(8):
                            act.wait_ge(s["v_mm"], u * 8 + (i + 1))
                            act.activation(vals[:, 2 * i:2 * i + 2, :, 0:DH0],
                                           u_ps[:, i % 4, :].rearrange("p (c h d) -> p c h d", c=2, h=4),
                                           ACT.Copy).then_inc(s["v_out"], 1)
                        for n in range(8):
                            for hh in range(2):
                                w = 2 * n + hh
                                act.wait_ge(s["sc_done"], u * 16 + (w + 2))
                                act.wait_ge(s["pv_done"], u * 16 + (max(w - 6 + 1, 0) + 1))
                                act.activation(prob[:, n % 3, hh, :], u_ps[:, w % 4, :],
                                               ACT.Exp).then_inc(s["exp_done"], 1)
                            if n == 2:
                                act.wait_ge(s["wv_in"], u * 16 + 32)
                                act.activation(wv_hi[:], wv_raw[:], ACT.Copy).then_inc(s["wv_hi_done"], 1)

            @block.tensor
            def _(pe):
                for n in ("sc_done", "pv_done", "k_mm", "norm_done"):
                    pe.sem_inc(s[n], 1)
                pe.wait_ge(s["vones"], 1)
                for b in range(NB):
                    for grp in range(NG):
                        pe.wait_ge(s["cstep"], b * 52 + (grp * 13 + 13))
                        for k in range(KD):
                            n = grp * KD + k
                            if n >= 4:
                                pe.wait_ge(s["cfull"], b * 16 + (n - 3))
                            for c in range(4):
                                ins = pe.transpose(u_ps[:, k, c * P:(c + 1) * P],
                                                   ctx_raw[:, grp % 2, c, k * P:(k + 1) * P], ident[:])
                            ins.then_inc(s["ctp"], 1)
                        pe.wait_ge(s["cfull"], b * 16 + (grp * KD + KD))
                        pe.sem_inc(s["ctx_free"], 1)

                    with pe.Fori(0, NQ) as g:
                        u = b * NQ + g
                        pe.wait_ge(s["csplit"], b * 32 + 32)
                        pe.wait_ge(s["wv_lo_done"], u + 1)
                        for i in range(8):
                            if i >= 4:
                                pe.wait_ge(s["v_out"], u * 8 + (i - 3))
                            for c in range(2):
                                rows = slice((2 * i + c) * P, (2 * i + c + 1) * P)
                                for k in range(KD):
                                    ins = split_matmul(pe, u_ps[:, i % 4, c * 256:(c + 1) * 256],
                                                       ctx_hi[:, k, rows], ctx_lo[:, k, rows],
                                                       wv_hi[:, k, :], wv_lo[:, k, :], k == 0, k == KD - 1)
                            ins.then_inc(s["v_mm"], 1)

                        def project(n):
                            pr, c = n // 4, n % 4
                            if n == 0:
                                pe.wait_ge(s["wk_lo_done"], u + 2)
                            if n >= 2:
                                pe.wait_ge(s["rope_done"], u * 32 + 4 * (n - 1))
                            for k in range(KD):
                                ins = split_matmul(pe, k_ps[:, n % 2, :], wk_hi[:, k, pr * P:(pr + 1) * P],
                                                   wk_lo[:, k, pr * P:(pr + 1) * P],
                                                   ctx_hi[:, k, c * 512:(c + 1) * 512],
                                                   ctx_lo[:, k, c * 512:(c + 1) * 512], k == 0, k == KD - 1)
                            ins.then_inc(s["k_mm"], 1)

                        def scores(n):
                            pr = n // 4
                            if n == 0:
                                pe.wait_ge(s["v_out"], u * 8 + 8)
                                pe.wait_ge(s["qcur_done"], u + 1)
                            pe.wait_ge(s["rope_done"], u * 32 + 4 * (n + 1))
                            for hh in range(2):
                                w = 2 * n + hh
                                if w >= 4:
                                    pe.wait_ge(s["exp_done"], u * 16 + (w - 3))
                                hd = 2 * pr + hh
                                for j in range(4):
                                    ins = pe.matmul(u_ps[:, w % 4, j * P:(j + 1) * P],
                                                    keys[:, n % 3, hh, j * P:(j + 1) * P],
                                                    q_cur[:, hd * P:(hd + 1) * P], start=True, stop=True)
                                ins.then_inc(s["sc_done"], 1)

                        def weigh(n):
                            pr, c = n // 4, n % 4
                            if c == 0:
                                pe.wait_ge(s["norm_done"], u * 4 + (2 * pr + 1))
                            for hh in range(2):
                                pe.wait_ge(s["clip_done"], u * 16 + (2 * n + hh + 1))
                                for j in range(4):
                                    ins = pe.matmul(o_ps[:, hh, 0:DH0 + 1], prob[:, n % 3, hh, j * P:(j + 1) * P],
                                                    vals[:, 4 * c + j, 2 * pr + hh, :],
                                                    start=(c == 0 and j == 0), stop=(c == 3 and j == 3))
                                ins.then_inc(s["pv_done"], 1)
                        for n in range(10):
                            if n < 8:
                                project(n)
                            if 1 <= n <= 8:
                                scores(n - 1)
                            if n >= 2:
                                weigh(n - 2)

        wo_in, aT_ready, aT_done, y_ready, r_done = (sem("x0o_" + n) for n in
                                                     ("wo_in", "aT_ready", "aT_done", "y_ready", "r_done"))
        with ExitStack() as st:
            wo = sb_in(st, "wo", [P, 8, D])
            bo = sb_in(st, "bo", [1, D])
            attn_T = sb_in(st, "attn_T", [P, 8, TOK])
            a_ps = ps_in(st, "a_ps", [P, 4, 2, TOK])
            y_ps = ps_in(st, "y_ps", [P, NB, D])
            block = st.enter_context(nc.Block())

            @block.sync
            def _(sp):
                sp.dma_start(wo[:], I["wo0"].rearrange("(k p) n -> p k n", p=P)).then_inc(wo_in, 16)
                sp.dma_start(bo[:], I["bo0"]).then_inc(wo_in, 16)

            @block.tensor
            def _(pe):
                for j in range(4):
                    for c in range(2):
                        for b in range(NB):
                            k = 2 * j + c
                            ins = pe.transpose(a_ps[:, j, c, b * P:(b + 1) * P],
                                               attn[:, b * 1024 + k * P:b * 1024 + (k + 1) * P], ident[:])
                    ins.then_inc(aT_ready, 1)
                pe.wait_ge(wo_in, 32)
                for b in range(NB):
                    pe.matmul(y_ps[:, b, :], ones_row[:], bo[:], start=True, stop=False)
                    for k in range(8):
                        if b == 0 and k % 2 == 0:
                            pe.wait_ge(aT_done, k // 2 + 1)
                        ins = pe.matmul(y_ps[:, b, :], attn_T[:, k, b * P:(b + 1) * P], wo[:, k, :],
                                        start=False, stop=(k == 7))
                    ins.then_inc(y_ready, 1)

            @block.scalar
            def _(act):
                for j in range(4):
                    act.wait_ge(aT_ready, j + 1)
                    act.activation(attn_T[:, 2 * j:2 * j + 2, :], a_ps[:, j, :, :], ACT.Copy).then_inc(aT_done, 1)

            @block.vector
            def _(dve):
                for b in range(NB):
                    dve.wait_ge(y_ready, b + 1)
                    dve.tensor_tensor(resid[:, b, :], y_ps[:, b, :], resid[:, b, :], ALU.add).then_inc(r_done, 1)


def self_attention(nc, I, env, tag, dh, layer):
    sem, sb_in, ps_in = env["sem"], env["sb_in"], env["ps_in"]
    resid, ident, ones_row, normed_T = env["resid"], env["ident"], env["ones_row"], env["normed_T"]
    per = P // dh
    KA = H // per
    W = H * dh
    NW = W // D
    scale = dh ** -0.5 if layer == 0 else dh ** 0.5
    wq, wk, wv, wp, rows, rope_c, rope_s, mask = (env[f"{tag}_{n}"] for n in
                                                  ("wq", "wk", "wv", "wp", "rows", "rc", "rs", "mask"))
    w_in, w_count = env[f"{tag}_w_in"], env[f"{tag}_w_count"]
    s = {n: sem(f"{tag}_{n}") for n in
         ("proj", "qk_out", "v_out", "rope", "qkT", "qkT_out", "score", "masked", "maxed", "shifted", "exped",
          "den", "pT", "pT_out", "pv", "normed", "aT", "aT_out", "y", "done")}

    env["layer_norm_T"](tag + "ln")
    with ExitStack() as st:
        qT = sb_in(st, tag + "qT", [P, KA, TOK])
        kT = sb_in(st, tag + "kT", [P, KA, TOK])
        v = sb_in(st, tag + "v", [P, NB, W])
        if layer == 0:
            turned = sb_in(st, tag + "turned", [P, NB, 2, D])
            part = sb_in(st, tag + "part", [P, NB, 4, 2, D // 2])
        sc = sb_in(st, tag + "sc", [P, NB, H * P])
        pT = sb_in(st, tag + "pT", [P, NB, H * P])
        stat = sb_in(st, tag + "stat", [P, 3, NB, H])
        attn = sb_in(st, tag + "attn", [P, NB, W])
        attn_T = sb_in(st, tag + "attn_T", [P, KA, TOK])
        bk = [ps_in(st, f"{tag}bk{b}", [P, 4, D]) for b in range(NB)]
        block = st.enter_context(nc.Block())

        def place(h):
            n = (h % per) * (H // per) + h // per
            return n // 4, (n % 4) * P

        @block.tensor
        def _(pe):
            pe.wait_ge(w_in, 16 * w_count)
            if layer == 0:
                for b in range(NB):
                    for m, w in enumerate((wq, wk, wv)):
                        pe.matmul(bk[b][:, m, :], ones_row[:], rows[:, m * D:(m + 1) * D], start=True, stop=False)
                        for k in range(KD):
                            ins = pe.matmul(bk[b][:, m, :], normed_T[:, k, b * P:(b + 1) * P], w[:, k, :],
                                            start=False, stop=(k == KD - 1))
                        ins.then_inc(s["proj"], 1)
                for b in range(NB):
                    pe.wait_ge(s["rope"], 6 * (b + 1))
                    for m in range(2):
                        for k in range(KA):
                            ins = pe.transpose(bk[b][:, m, k * P:(k + 1) * P], turned[:, b, m, k * P:(k + 1) * P],
                                               ident[:])
                        ins.then_inc(s["qkT"], 1)
            else:
                for m, w in enumerate((wq, wk)):
                    for n in range(KA):
                        for k in range(KD):
                            ins = pe.matmul(bk[m][:, n // 2, (n % 2) * TOK:(n % 2 + 1) * TOK],
                                            w[:, k, n * P:(n + 1) * P], normed_T[:, k, :],
                                            start=(k == 0), stop=(k == KD - 1))
                        if n % 2:
                            ins.then_inc(s["qkT"], 1)
                for b in range(NB):
                    for m in range(NW):
                        pe.wait_ge(s["qkT_out"], 4 * b + m + 1)
                        for k in range(KD):
                            ins = pe.matmul(bk[b][:, m, :], normed_T[:, k, b * P:(b + 1) * P],
                                            wv[:, k, m * D:(m + 1) * D], start=(k == 0), stop=(k == KD - 1))
                        ins.then_inc(s["proj"], 1)
            for b in range(NB):
                if layer == 0:
                    pe.wait_ge(s["qkT_out"], 2 * (b + 1))
                    pe.wait_ge(s["v_out"], b + 1)
                else:
                    pe.wait_ge(s["qkT_out"], 8)
                    pe.wait_ge(s["v_out"], NW * (b + 1))
                for h in sorted(range(H), key=lambda h: place(h)):
                    bank, col = place(h)
                    r = slice((h % per) * dh, (h % per + 1) * dh)
                    ins = pe.matmul(bk[b][:, bank, col:col + P], qT[r, h // per, b * P:(b + 1) * P],
                                    kT[r, h // per, b * P:(b + 1) * P], start=True, stop=True)
                    if col == 3 * P:
                        ins.then_inc(s["score"], 1)
            for b in range(NB):
                pe.wait_ge(s["exped"], b + 1)
                for n in range(H):
                    ins = pe.transpose(bk[b][:, n // 4, (n % 4) * P:(n % 4 + 1) * P], sc[:, b, n * P:(n + 1) * P],
                                       ident[:])
                    if n % 4 == 3:
                        ins.then_inc(s["pT"], 1)
            for b in range(NB):
                pe.wait_ge(s["pT_out"], 4 * (b + 1))
                for h in range(H):
                    bank, col = place(h)
                    at = bank * 4 * P + col
                    ins = pe.matmul(bk[b][:, h * dh // D, h * dh % D:h * dh % D + dh], pT[:, b, at:at + P],
                                    v[:, b, h * dh:(h + 1) * dh], start=True, stop=True)
                ins.then_inc(s["pv"], 1)
            for b in range(NB):
                pe.wait_ge(s["normed"], b + 1)
                for k in range(KA):
                    ins = pe.transpose(bk[b][:, 2 + k // 4, (k % 4) * P:(k % 4 + 1) * P],
                                       attn[:, b, k * P:(k + 1) * P], ident[:])
                ins.then_inc(s["aT"], 1)
            for b in range(NB):
                pe.wait_ge(s["aT_out"], b + 1)
                if layer == 0:
                    pe.matmul(bk[b][:, 0, :], ones_row[:], rows[:, 3 * D:4 * D], start=True, stop=False)
                for k in range(KA):
                    ins = pe.matmul(bk[b][:, 0, :], attn_T[:, k, b * P:(b + 1) * P], wp[:, k, :],
                                    start=(k == 0 and layer == 1), stop=(k == KA - 1))
                ins.then_inc(s["y"], 1)

        @block.scalar
        def _(act):
            if layer == 0:
                for b in range(NB):
                    act.wait_ge(s["proj"], 3 * b + 3)
                    act.activation(v[:, b, :], bk[b][:, 2, :], ACT.Copy).then_inc(s["v_out"], 1)
                for b in range(NB):
                    for m, dst in enumerate((qT, kT)):
                        act.wait_ge(s["qkT"], 2 * b + m + 1)
                        act.activation(dst[:, :, b * P:(b + 1) * P],
                                       bk[b][:, m, :].rearrange("p (k t) -> p k t", k=KA),
                                       ACT.Copy).then_inc(s["qkT_out"], 1)
            else:
                for m, dst in enumerate((qT, kT)):
                    for n in range(4):
                        act.wait_ge(s["qkT"], 4 * m + n + 1)
                        act.activation(dst[:, 2 * n:2 * n + 2, :],
                                       bk[m][:, n, :].rearrange("p (k t) -> p k t", k=2),
                                       ACT.Copy).then_inc(s["qkT_out"], 1)
                for b in range(NB):
                    for m in range(NW):
                        act.wait_ge(s["proj"], NW * b + m + 1)
                        act.activation(v[:, b, m * D:(m + 1) * D], bk[b][:, m, :], ACT.Copy).then_inc(s["v_out"], 1)
            for b in range(NB):
                act.wait_ge(s["shifted"], b + 1)
                act.activation(sc[:, b, :], sc[:, b, :], ACT.Exp, scale=scale).then_inc(s["exped"], 1)
            for b in range(NB):
                for n in range(4):
                    act.wait_ge(s["pT"], 4 * b + n + 1)
                    act.activation(pT[:, b, n * D:(n + 1) * D], bk[b][:, n, :], ACT.Copy).then_inc(s["pT_out"], 1)
            for b in range(NB):
                act.wait_ge(s["aT"], b + 1)
                act.activation(attn_T[:, :, b * P:(b + 1) * P],
                               bk[b][:, 2:4, :].rearrange("p u (k t) -> p (u k) t", t=P)[:, 0:KA, :],
                               ACT.Copy).then_inc(s["aT_out"], 1)

        @block.vector
        def _(dve):
            if layer == 0:
                dve.wait_ge(w_in, 16 * w_count)
                cc, ss = (t[:].rearrange("p (m n) -> p m n", m=2) for t in (rope_c, rope_s))
                for b in range(NB):
                    dve.wait_ge(s["proj"], 3 * b + 2)
                    pairs = bk[b][:, 0:2, :].rearrange("p m (n two) -> p m n two", two=2)
                    even, odd = pairs[:, :, :, 0], pairs[:, :, :, 1]
                    for i, (a, t) in enumerate(((even, cc), (odd, ss), (even, ss), (odd, cc))):
                        dve.tensor_tensor(part[:, b, i, :, :], a, t, ALU.mult).then_inc(s["rope"], 1)
                    dve.wait_ge(s["rope"], 6 * b + 4)
                    to = turned[:, b, :, :].rearrange("p m (n two) -> p m n two", two=2)
                    dve.tensor_tensor(to[:, :, :, 0], part[:, b, 0, :, :], part[:, b, 1, :, :],
                                      ALU.subtract).then_inc(s["rope"], 1)
                    dve.tensor_tensor(to[:, :, :, 1], part[:, b, 2, :, :], part[:, b, 3, :, :],
                                      ALU.add).then_inc(s["rope"], 1)
            else:
                dve.wait_ge(w_in, 16 * w_count)
            for b in range(NB):
                heads = sc[:, b, :].rearrange("p (h t) -> p h t", h=H)
                for n in range(4):
                    dve.wait_ge(s["score"], 4 * b + n + 1)
                    dve.tensor_tensor(sc[:, b, n * D:(n + 1) * D], bk[b][:, n, :], mask[:],
                                      ALU.add).then_inc(s["masked"], 1)
                dve.wait_ge(s["masked"], 4 * (b + 1))
                dve.tensor_reduce(stat[:, 0, b, :], heads, AX.X, ALU.max).then_inc(s["maxed"], 1)
                dve.wait_ge(s["maxed"], b + 1)
                dve.tensor_tensor(heads, heads, stat[:, 0, b, :].unsqueeze(2).broadcast_to([P, H, P]),
                                  ALU.subtract).then_inc(s["shifted"], 1)
            for b in range(NB):
                dve.wait_ge(s["exped"], b + 1)
                dve.tensor_reduce(stat[:, 1, b, :], sc[:, b, :].rearrange("p (h t) -> p h t", h=H), AX.X,
                                  ALU.add).then_inc(s["den"], 1)
                dve.wait_ge(s["den"], 2 * b + 1)
                dve.reciprocal(stat[:, 2, b, :], stat[:, 1, b, :]).then_inc(s["den"], 1)
            for b in range(NB):
                dve.wait_ge(s["pv"], b + 1)
                dve.wait_ge(s["den"], 2 * b + 2)
                inv = stat[:, 2, b, :].rearrange("p (r g) -> p g r", r=per).unsqueeze(3).broadcast_to([P, KA, per, dh])
                o = bk[b][:, 0:NW, :].rearrange("p u n -> p (u n)").rearrange("p (g r d) -> p g r d", g=KA, r=per)
                dve.tensor_tensor(attn[:, b, :].rearrange("p (g r d) -> p g r d", g=KA, r=per), o, inv,
                                  ALU.mult).then_inc(s["normed"], 1)
            for b in range(NB):
                dve.wait_ge(s["y"], b + 1)
                dve.tensor_tensor(resid[:, b, :], bk[b][:, 0, :], resid[:, b, :], ALU.add).then_inc(s["done"], 1)


def sign_layer(nc, I, env):
    sem, sb_in, ps_in = env["sem"], env["sb_in"], env["ps_in"]
    resid, normed_T = env["resid"], env["normed_T"]
    w, w_in, w_need = env["sgn_w"], env["sgn_w_in"], env["sgn_w_need"]
    signed, y_ready, done = sem("sg_signed"), sem("sg_y"), sem("sg_done")
    with nc.Block() as block:
        @block.scalar
        def _(act):
            act.wait_ge(w_in, w_need)
            act.activation(w[:], w[:], ACT.Sign).then_inc(signed, 1)
    env["layer_norm_T"]("sgln")
    with ExitStack() as st:
        y_ps = ps_in(st, "sg_y_ps", [P, NB, D])
        block = st.enter_context(nc.Block())

        @block.tensor
        def _(pe):
            pe.wait_ge(signed, 1)
            for b in range(NB):
                for k in range(KD):
                    ins = pe.matmul(y_ps[:, b, :], normed_T[:, k, b * P:(b + 1) * P], w[:, k, :],
                                    start=(k == 0), stop=(k == KD - 1))
                ins.then_inc(y_ready, 1)

        @block.vector
        def _(dve):
            for b in range(NB):
                dve.wait_ge(y_ready, b + 1)
                dve.tensor_tensor(resid[:, b, :], y_ps[:, b, :], resid[:, b, :], ALU.add).then_inc(done, 1)


def cross_attention_masked(nc, I, env):
    sem, sb_in, ps_in = env["sem"], env["sb_in"], env["ps_in"]
    resid, ident, ones_row, normed_T = env["resid"], env["ident"], env["ones_row"], env["normed_T"]
    wo, wo_row, w_in, w_need = env["wo1"], env["wo1_row"], env["wo1_in"], env["wo1_need"]
    s = {n: sem("x1_" + n) for n in
         ("k_in", "v_in0", "v_in1", "m_in", "k_hi", "k_lo", "zeroed", "q_hi", "q_lo", "score", "masked",
          "top", "topped", "exped", "den", "pT", "pT_out_a", "pT_out_v", "pv", "normed", "aT", "aT_out", "y",
          "act_y", "done")}
    SC0, PV0 = 17, 5
    env["layer_norm_T"]("x1ln")
    q_view = normed_T[:].rearrange("p k t -> p (k t)")
    with ExitStack() as st:
        attn = sb_in(st, "x1_attn", [P, NB, D])
        attn_T = sb_in(st, "x1_attn_T", [P, KD, TOK])
        attn_flat = attn[:].rearrange("p b n -> p (b n)")
        with ExitStack() as st2:
            mask = sb_in(st2, "x1_mask", [P, NB, S])
            k_raw = sb_in(st2, "x1_k_raw", [P, S])
            k_hi = sb_in(st2, "x1_k_hi", [P, 2, S], F32R)
            k_lo = sb_in(st2, "x1_k_lo", [P, 2, S], F32R)
            val = sb_in(st2, "x1_val", [P, 2, NCH, P])
            q_hi = sb_in(st2, "x1_q_hi", [P, 2, 4, P], F32R)
            q_lo = sb_in(st2, "x1_q_lo", [P, 2, 4, P], F32R)
            sc = sb_in(st2, "x1_sc", [P, 2, S])
            pT = sb_in(st2, "x1_pT", [P, 4, 512])
            tops = sb_in(st2, "x1_tops", [P, 2, 4])
            gate = sb_in(st2, "x1_gate", [1, 3, 4])
            negtop = sb_in(st2, "x1_negtop", [P, 2])
            den = sb_in(st2, "x1_den", [P, 2])
            rden = sb_in(st2, "x1_rden", [P, 2])
            s_ps = ps_in(st2, "x1_s_ps", [P, 4, 512])
            t_ps = ps_in(st2, "x1_t_ps", [P, 2, 512])
            o_ps = ps_in(st2, "x1_o_ps", [P, 2, 512])
            block = st2.enter_context(nc.Block())


            @block.sync
            def _(sp):
                sp.dma_start(mask[:], I["mask"].rearrange("b p n -> p b n")).then_inc(s["m_in"], 16)
                for b in range(NB):
                    with sp.Fori(0, 2) as i:
                        for r in range(2):
                            G = b * 4 + i * 2 + r
                            sp.wait_ge(s["k_lo"], G + 1)
                            sp.dma_start(k_raw[:], I["ctx_T"][bass.ds(G * P, P), :]).then_inc(s["k_in"], 16)
                            sp.wait_ge(s["pv"], G * 4 + 1)
                            sp.dma_start(val[:, r, :, :], I["ctx_heads"][bass.ds(G * P, P), :]
                                         .rearrange("p (c n) -> p c n", c=NCH)).then_inc(s[f"v_in{r}"], 16)

            @block.gpsimd
            def _(pool):
                pool.memset(q_hi[:].bitcast(F32), 0.0).then_inc(s["zeroed"], 1)
                pool.memset(q_lo[:].bitcast(F32), 0.0).then_inc(s["zeroed"], 1)
                pool.memset(gate[:], 0.0).then_inc(s["zeroed"], 1)
                pool.sem_inc(s["k_lo"], 1)
                for b in range(NB):
                    with pool.Fori(0, 2) as i:
                        for r in range(2):
                            G = b * 4 + i * 2 + r
                            pool.wait_ge(s["k_hi"], G + 1)
                            pool.wait_ge(s["score"], G * 16 + 1)
                            pool.tensor_tensor(k_lo[:, r, :], k_raw[:], k_hi[:, r, :],
                                               ALU.subtract).then_inc(s["k_lo"], 1)

            @block.vector
            def _(dve):
                dve.wait_ge(s["zeroed"], 3)
                dve.wait_ge(s["m_in"], 16)
                for b in range(NB):
                    with dve.Fori(0, 2) as i:
                        def prepare(r):
                            G = b * 4 + i * 2 + r
                            dve.wait_ge(s["k_in"], 16 * G + 16)
                            dve.wait_ge(s["score"], G * 16 + 1)
                            dve.tensor_copy(k_hi[:, r, :], k_raw[:]).then_inc(s["k_hi"], 1)
                            for j in range(4):
                                rows = slice(32 * j, 32 * j + 32)
                                src = q_view[rows, bass.ds((i * 2 + r) * TOK + b * P, P)]
                                dve.tensor_copy(q_hi[rows, r, j, :], src).then_inc(s["q_hi"], 1)
                            for j in range(4):
                                rows = slice(32 * j, 32 * j + 32)
                                src = q_view[rows, bass.ds((i * 2 + r) * TOK + b * P, P)]
                                dve.wait_ge(s["q_hi"], G * 4 + (j + 1))
                                dve.tensor_tensor(q_lo[rows, r, j, :], src, q_hi[rows, r, j, :],
                                                  ALU.subtract).then_inc(s["q_lo"], 1)

                        def top(t):
                            hd = b * 16 + i * 8 + t
                            dve.wait_ge(s["pv"], hd + (PV0 - 1))
                            for c in range(4):
                                dve.wait_ge(s["score"], hd * 4 + (SC0 + c + 1))
                                dve.tensor_copy(gate[0:1, t % 2, c:c + 1], gate[0:1, 2, 0:1])
                                dve.tensor_tensor_reduce(sc[:, t % 2, c * 512:(c + 1) * 512], s_ps[:, c, :],
                                                         mask[:, b, c * 512:(c + 1) * 512], 1.0, -3.0e38, ALU.add,
                                                         ALU.max, tops[:, t % 2, c:c + 1]).then_inc(s["masked"], 1)
                            dve.wait_ge(s["masked"], hd * 4 + 4)
                            dve.tensor_reduce(negtop[:, t % 2:t % 2 + 1], tops[:, t % 2, :], AX.X, ALU.max,
                                              negate=True).then_inc(s["top"], 1)

                        def evacuate(t):
                            hd = b * 16 + i * 8 + t
                            dve.wait_ge(s["pT"], hd * 4 + 4)
                            dve.tensor_copy(pT[:, 3, :], t_ps[:, 1, :]).then_inc(s["pT_out_v"], 1)

                        def normalise(t):
                            hd = b * 16 + i * 8 + t
                            dve.wait_ge(s["exped"], hd + 1)
                            dve.reciprocal(rden[:, t % 2:t % 2 + 1], den[:, t % 2:t % 2 + 1]).then_inc(s["den"], 1)
                            dve.wait_ge(s["den"], hd + 1)
                            dve.wait_ge(s["pv"], hd + (PV0 + 1))
                            dve.tensor_scalar(attn_flat[:, bass.ds(b * D + (i * 8 + t) * DHS, DHS)],
                                              o_ps[:, t % 2, 0:DHS], rden[:, t % 2:t % 2 + 1], None,
                                              ALU.mult).then_inc(s["normed"], 1)
                        prepare(0)
                        top(0)
                        prepare(1)
                        for t in range(8):
                            if t + 1 < 8:
                                top(t + 1)
                            evacuate(t)
                            normalise(t)

            @block.scalar
            def _(act):
                for b in range(NB):
                    with act.Fori(0, 2) as i:
                        for t in range(8):
                            hd = b * 16 + i * 8 + t
                            act.wait_ge(s["top"], hd + 1)
                            act.wait_ge(s["normed"], hd + 1)
                            act.activation(sc[:, t % 2, :], sc[:, t % 2, :], ACT.Exp, bias=negtop[:, t % 2:t % 2 + 1],
                                           accum_out=den[:, t % 2:t % 2 + 1]).then_inc(s["exped"], 1)
                            for c in range(3):
                                act.wait_ge(s["pT"], hd * 4 + (c + 1))
                                act.wait_ge(s["pv"], hd + PV0)
                                act.activation(pT[:, c, :], t_ps[:, c % 2, :], ACT.Copy).then_inc(s["pT_out_a"], 1)

            @block.tensor
            def _(pe):
                pe.sem_inc(s["score"], SC0)
                pe.sem_inc(s["pv"], PV0)
                pe.sem_inc(s["normed"], 2)
                for b in range(NB):
                    with pe.Fori(0, 2) as i:
                        def scores(t):
                            hd = b * 16 + i * 8 + t
                            G, r, j = b * 4 + i * 2 + t // 4, t // 4, t % 4
                            if j == 0:
                                pe.wait_ge(s["k_lo"], G + 2)
                                pe.wait_ge(s["q_lo"], G * 4 + 4)
                            for c in range(4):
                                if t:
                                    pe.wait_ge(s["masked"], (hd - 1) * 4 + (c + 1))
                                ins = split_matmul(pe, s_ps[:, c, :], q_hi[:, r, j, :], q_lo[:, r, j, :],
                                                   k_hi[:, r, c * 512:(c + 1) * 512],
                                                   k_lo[:, r, c * 512:(c + 1) * 512], True, True)
                                ins.then_inc(s["score"], 1)

                        def turn(t, c):
                            hd = b * 16 + i * 8 + t
                            if c == 0:
                                pe.wait_ge(s["exped"], hd + 1)
                            if c >= 2:
                                pe.wait_ge(s["pT_out_a"], hd * 3 + (c - 1))
                            for k in range(4):
                                ins = pe.transpose(t_ps[:, c % 2, k * P:(k + 1) * P],
                                                   sc[:, t % 2, (4 * c + k) * P:(4 * c + k + 1) * P], ident[:])
                            ins.then_inc(s["pT"], 1)

                        def weigh(t, c):
                            hd = b * 16 + i * 8 + t
                            r, j = t // 4, t % 4
                            if c == 0:
                                pe.wait_ge(s["normed"], hd + 1)
                                if j == 0:
                                    pe.wait_ge(s[f"v_in{r}"], (b * 2 + i) * 16 + 16)
                            if c < 3:
                                pe.wait_ge(s["pT_out_a"], hd * 3 + (c + 1))
                            else:
                                pe.wait_ge(s["pT_out_v"], hd + 1)
                            for k in range(4):
                                ins = pe.matmul(o_ps[:, t % 2, 0:DHS], pT[:, c, k * P:(k + 1) * P],
                                                val[:, r, 4 * c + k, j * DHS:(j + 1) * DHS],
                                                start=(c == 0 and k == 0), stop=(c == 3 and k == 3))
                            if c == 3:
                                ins.then_inc(s["pv"], 1)
                        for t in range(9):
                            if t < 8:
                                scores(t)
                            if t:
                                turn(t - 1, 0)
                                turn(t - 1, 1)
                                weigh(t - 1, 0)
                                turn(t - 1, 2)
                                weigh(t - 1, 1)
                                turn(t - 1, 3)
                                weigh(t - 1, 2)
                                weigh(t - 1, 3)
        with ExitStack() as st2:
            a_ps = ps_in(st2, "x1_a_ps", [P, 2, 2, TOK])
            y_ps = ps_in(st2, "x1_y_ps", [P, NB, D])
            y = sb_in(st2, "x1_y", [P, NB, D])
            block = st2.enter_context(nc.Block())

            @block.tensor
            def _(pe):
                for n in range(2):
                    for c in range(2):
                        for b in range(NB):
                            k = 2 * n + c
                            ins = pe.transpose(a_ps[:, n, c, b * P:(b + 1) * P], attn[:, b, k * P:(k + 1) * P],
                                               ident[:])
                    ins.then_inc(s["aT"], 1)
                pe.wait_ge(w_in, w_need)
                for b in range(NB):
                    pe.matmul(y_ps[:, b, :], ones_row[:], wo_row[:], start=True, stop=False)
                    for k in range(KD):
                        if b == 0 and k % 2 == 0:
                            pe.wait_ge(s["aT_out"], k // 2 + 1)
                        ins = pe.matmul(y_ps[:, b, :], attn_T[:, k, b * P:(b + 1) * P], wo[:, k, :],
                                        start=False, stop=(k == KD - 1))
                    ins.then_inc(s["y"], 1)

            @block.scalar
            def _(act):
                for n in range(2):
                    act.wait_ge(s["aT"], n + 1)
                    act.activation(attn_T[:, 2 * n:2 * n + 2, :], a_ps[:, n, :, :], ACT.Copy).then_inc(s["aT_out"], 1)
                for b in range(NB):
                    act.wait_ge(s["y"], b + 1)
                    act.activation(y[:, b, :], y_ps[:, b, :], ACT.Relu).then_inc(s["act_y"], 1)

            @block.vector
            def _(dve):
                for b in range(NB):
                    dve.wait_ge(s["act_y"], b + 1)
                    dve.tensor_tensor(resid[:, b, :], y[:, b, :], resid[:, b, :], ALU.add).then_inc(s["done"], 1)


def experts(nc, I, env):
    sem, sb_in, ps_in = env["sem"], env["sb_in"], env["ps_in"]
    resid, normed_T, ones_row, ident = env["resid"], env["normed_T"], env["ones_row"], env["ident"]
    w1_raw, w2_raw, s1, s2 = env["w1_raw"], env["w2_raw"], env["w1_in"], env["w2_in"]
    E, NP = E_MOE, 4
    s = {n: sem("mo_" + n) for n in
         ("small_in", "logit", "step", "exp", "rT", "rT_out", "bias", "acc", "w1_hi", "w1_lo", "w2_hi", "w2_lo",
          "h_mm", "gelu", "h_hi", "h_lo", "y_mm", "x_hi", "x_lo", "b1", "r_cur", "added")}
    env["layer_norm_T"]("moln")
    with ExitStack() as st:
        wr = sb_in(st, "mo_wr", [P, KD, E])
        br = sb_in(st, "mo_br", [1, E])
        b2 = sb_in(st, "mo_b2", [E, D])
        b1 = sb_in(st, "mo_b1", [P, E * 16])
        b1_cur = sb_in(st, "mo_b1_cur", [P, 2, 4])
        before = sb_in(st, "mo_before", [P, E * E])
        logit = sb_in(st, "mo_logit", [P, NB, E])
        cmp_a = sb_in(st, "mo_cmp_a", [P, NB, E, E])
        cmp_b = sb_in(st, "mo_cmp_b", [P, NB, E, E])
        rank = sb_in(st, "mo_rank", [P, NB, E])
        stat = sb_in(st, "mo_stat", [P, 3, NB])
        route = sb_in(st, "mo_route", [P, NB, E])
        r_cur = sb_in(st, "mo_r_cur", [P, NB])
        route_T = sb_in(st, "mo_route_T", [E, NB, P])
        x_hi = sb_in(st, "mo_x_hi", [P, KD, TOK], F32R)
        x_lo = sb_in(st, "mo_x_lo", [P, KD, TOK], F32R)
        w1_hi = sb_in(st, "mo_w1_hi", [P, 2, KD, 512], F32R)
        w1_lo = sb_in(st, "mo_w1_lo", [P, 2, KD, 512], F32R)
        w2_hi = sb_in(st, "mo_w2_hi", [P, 2, NP, D], F32R)
        w2_lo = sb_in(st, "mo_w2_lo", [P, 2, NP, D], F32R)
        hid = sb_in(st, "mo_hid", [P, 2, NP, TOK])
        h_hi = sb_in(st, "mo_h_hi", [P, 2, NP, TOK], F32R)
        h_lo = sb_in(st, "mo_h_lo", [P, 2, NP, TOK], F32R)
        h_ps = ps_in(st, "mo_h_ps", [P, 4, 512])
        y_ps = ps_in(st, "mo_y_ps", [P, 2, NB, D])
        with nc.Block() as block:
            @block.gpsimd
            def _(pool):
                for dst, name in ((wr[:], "wr"), (br[:], "br"), (b2[:], "b2"), (b1[:], "b1"), (before[:], "before")):
                    pool.dma_start(dst, I[name]).then_inc(s["small_in"], 16)

            @block.tensor
            def _(pe):
                pe.wait_ge(s["small_in"], 16 * 5)
                for b in range(NB):
                    lg = y_ps[:, 0, b, 0:E]
                    pe.matmul(lg, ones_row[:], br[:], start=True, stop=False)
                    for k in range(KD):
                        ins = pe.matmul(lg, normed_T[:, k, b * P:(b + 1) * P], wr[:, k, :], start=False,
                                        stop=(k == KD - 1))
                ins.then_inc(s["logit"], 1)
                pe.wait_ge(s["step"], 17)
                for b in range(NB):
                    ins = pe.transpose(h_ps[0:E, 0, b * P:(b + 1) * P], route[:, b, :], ident[:])
                ins.then_inc(s["rT"], 1)
                pe.wait_ge(s["rT_out"], 1)
                for b in range(NB):
                    ins = pe.matmul(y_ps[:, 1, b, :], route_T[:, b, :], b2[:], start=True, stop=True)
                ins.then_inc(s["bias"], 1)

            @block.scalar
            def _(act):
                act.activation(x_hi[:], normed_T[:], ACT.Copy).then_inc(s["x_hi"], 1)
                act.wait_ge(s["step"], 10)
                act.activation(route[:], logit[:], ACT.Exp).then_inc(s["exp"], 1)

            @block.vector
            def _(dve):
                dve.wait_ge(s["x_hi"], 1)
                dve.tensor_tensor(x_lo[:], normed_T[:], x_hi[:], ALU.subtract).then_inc(s["x_lo"], 1)
                step = Chain(dve, s["step"])
                dve.wait_ge(s["logit"], 1)
                step(dve.tensor_copy(logit[:], y_ps[:, 0, :, 0:E]))
                for b in range(NB):
                    other = logit[:, b, :].unsqueeze(1).broadcast_to([P, E, E])
                    own = logit[:, b, :].unsqueeze(2).broadcast_to([P, E, E])
                    dve.tensor_tensor(cmp_a[:, b, :, :], other, own, ALU.is_gt).then_inc(s["step"], 1)
                    dve.tensor_tensor(cmp_b[:, b, :, :], other, own, ALU.is_equal).then_inc(s["step"], 1)
                step.n += 4
                dve.wait_ge(s["step"], step.n)
                low = before[:].rearrange("p (e f) -> p e f", e=E).unsqueeze(1).broadcast_to([P, NB, E, E])
                flat = lambda t: t[:].rearrange("p b e f -> p (b e) f")
                step(dve.tensor_tensor(cmp_b[:], cmp_b[:], low, ALU.mult))
                step(dve.tensor_tensor(flat(cmp_a), flat(cmp_a), flat(cmp_b), ALU.add))
                step(dve.tensor_reduce(rank[:].rearrange("p b e -> p (b e)"), flat(cmp_a), AX.X, ALU.add))
                step(dve.tensor_reduce(stat[:, 0, :], logit[:], AX.X, ALU.max))
                step(dve.tensor_tensor(logit[:], logit[:], stat[:, 0, :].unsqueeze(2).broadcast_to([P, NB, E]),
                                       ALU.subtract))
                dve.wait_ge(s["exp"], 1)
                step(dve.tensor_scalar(rank[:], rank[:], 2.0, None, ALU.is_lt))
                step(dve.tensor_tensor(route[:], route[:], rank[:], ALU.mult))
                step(dve.tensor_reduce(stat[:, 1, :], route[:], AX.X, ALU.add))
                step(dve.reciprocal(stat[:, 2, :], stat[:, 1, :]))
                step(dve.tensor_tensor(route[:], route[:], stat[:, 2, :].unsqueeze(2).broadcast_to([P, NB, E]),
                                       ALU.mult))
                step(dve.memset(r_cur[:], 0.0))
                step(dve.memset(b1_cur[:], 0.0))
                assert step.n == 17
                dve.wait_ge(s["rT"], 1)
                dve.tensor_copy(route_T[:], h_ps[0:E, 0, 0:TOK].rearrange("e (b t) -> e b t", b=NB))\
                    .then_inc(s["rT_out"], 1)
                dve.wait_ge(s["bias"], 1)
                for b in range(NB):
                    dve.tensor_tensor(resid[:, b, :], y_ps[:, 1, b, :], resid[:, b, :], ALU.add).then_inc(s["acc"], 1)

        block = st.enter_context(nc.Block())

        @block.sync
        def _(sp):
            def load(e, j):
                U = e * NU + j
                sp.wait_ge(s["w1_lo"], U - 1)
                sp.dma_start(w1_raw[:, j % 2, :, :], I["w1"][bass.ds(U * P, P), :]
                             .rearrange("p (k n) -> p k n", k=KD)).then_inc(s1[j % 2], 16)
                sp.wait_ge(s["w2_lo"], U - 1)
                sp.dma_start(w2_raw[:, j % 2, :, :], I["w2"][bass.ds(U * P, P), :]
                             .rearrange("p (k n) -> p k n", k=NP)).then_inc(s2[j % 2], 16)
            for j in (2, 3):
                load(0, j)
            with sp.Fori(1, E) as e:
                for j in range(NU):
                    load(e, j)

        @block.scalar
        def _(act):
            def high1(e, j, first=False):
                U, r = e * NU + j, j % 2
                act.wait_ge(s1[r], e * 32 + 16 * (j // 2 + 1))
                if not first:
                    act.wait_ge(s["h_mm"], U * NP - NP)
                act.activation(w1_hi[:, r, :, :], w1_raw[:, r, :, :], ACT.Copy).then_inc(s["w1_hi"], 1)

            def high2(e, j, first=False):
                U, r = e * NU + j, j % 2
                act.wait_ge(s2[r], e * 32 + 16 * (j // 2 + 1))
                if not first:
                    act.wait_ge(s["y_mm"], U - 1)
                act.activation(w2_hi[:, r, :, :], w2_raw[:, r, :, :], ACT.Copy).then_inc(s["w2_hi"], 1)

            def gelu(e, j):
                U, r = e * NU + j, j % 2
                act.wait_ge(s["b1"], U + 1)
                act.wait_ge(s["h_lo"], U + 1)
                for n in range(NP):
                    act.wait_ge(s["h_mm"], U * NP + (n // 2 * 2 + 2))
                    act.activation(hid[:, r, n, :], h_ps[:, 2 * r + n // 2, (n % 2) * TOK:(n % 2 + 1) * TOK],
                                   ACT.Gelu_apprx_tanh, bias=b1_cur[:, r, n:n + 1]).then_inc(s["gelu"], 1)

            high1(0, 0, True)
            high1(0, 1, True)
            high2(0, 0, True)

            def expert(e, first=False, last=False):
                for j in range(NU):
                    gelu(e, j)
                    if not (last and j >= 2):
                        high1(e, j + 2)
                    if not (last and j == 3):
                        high2(e, j + 1, first and j == 0)
            expert(0, first=True)
            with act.Fori(1, E - 1) as e:
                expert(e)
            expert(E - 1, last=True)

        @block.vector
        def _(dve):
            dve.sem_inc(s["h_lo"], 2)
            dve.sem_inc(s["added"], 1)

            def low1(e, j):
                U, r = e * NU + j, j % 2
                dve.wait_ge(s["w1_hi"], U + 1)
                dve.tensor_tensor(w1_lo[:, r, :, :], w1_raw[:, r, :, :], w1_hi[:, r, :, :],
                                  ALU.subtract).then_inc(s["w1_lo"], 1)

            def low2(e, j):
                U, r = e * NU + j, j % 2
                dve.wait_ge(s["w2_hi"], U + 1)
                dve.tensor_tensor(w2_lo[:, r, :, :], w2_raw[:, r, :, :], w2_hi[:, r, :, :],
                                  ALU.subtract).then_inc(s["w2_lo"], 1)

            def bias(e, j, first):
                U = e * NU + j
                if not first:
                    dve.wait_ge(s["gelu"], U * NP - NP)
                dve.tensor_copy(b1_cur[:, j % 2, :], b1[:, bass.ds(U * NP, NP)]).then_inc(s["b1"], 1)

            def split(e, j, first):
                U, r = e * NU + j, j % 2
                if not first:
                    dve.wait_ge(s["y_mm"], U - 1)
                dve.wait_ge(s["gelu"], U * NP + NP)
                dve.tensor_copy(h_hi[:, r, :, :], hid[:, r, :, :]).then_inc(s["h_hi"], 1)
                dve.wait_ge(s["h_hi"], U + 1)
                dve.tensor_tensor(h_lo[:, r, :, :], hid[:, r, :, :], h_hi[:, r, :, :],
                                  ALU.subtract).then_inc(s["h_lo"], 1)

            def combine(e, par):
                dve.tensor_copy(r_cur[:], route[:, :, bass.ds(e, 1)].rearrange("p b o -> p (b o)"))\
                    .then_inc(s["r_cur"], 1)
                dve.wait_ge(s["r_cur"], e + 1)
                dve.wait_ge(s["y_mm"], e * NU + NU)
                for b in range(NB):
                    dve.scalar_tensor_tensor(resid[:, b, :], y_ps[:, par, b, :], r_cur[:, b:b + 1],
                                             resid[:, b, :], ALU.mult, ALU.add).then_inc(s["added"], 1)
                dve.wait_ge(s["added"], e * NB + (NB + 1))
            low1(0, 0)
            low1(0, 1)
            low2(0, 0)
            bias(0, 0, True)

            def unit(e, j, first=False, last=False):
                if not (last and j == 3):
                    bias(e, j + 1, first and j == 0)
                split(e, j, first and j < 2)
                if not (last and j >= 2):
                    low1(e, j + 2)
                if not (last and j == 3):
                    low2(e, j + 1)
            for j in range(NU):
                unit(0, j, first=True)
            with dve.Fori(0, E // 2 - 1) as i:
                for half in range(2):
                    e = i * 2 + half
                    for j in range(NU):
                        unit(e + 1, j)
                        if j == 0:
                            combine(e, half)
            for j in range(NU):
                unit(E - 1, j, last=True)
                if j == 0:
                    combine(E - 2, 0)
            combine(E - 1, 1)

        @block.tensor
        def _(pe):
            def hidden(e, j, first=False):
                U, r = e * NU + j, j % 2
                pe.wait_ge(s["w1_lo"], U + 1)
                if not first:
                    pe.wait_ge(s["gelu"], U * NP - NP)
                for n in range(NP):
                    for k in range(KD):
                        ins = split_matmul(pe, h_ps[:, 2 * r + n // 2, (n % 2) * TOK:(n % 2 + 1) * TOK],
                                           w1_hi[:, r, k, n * P:(n + 1) * P], w1_lo[:, r, k, n * P:(n + 1) * P],
                                           x_hi[:, k, :], x_lo[:, k, :], k == 0, k == KD - 1)
                    ins.then_inc(s["h_mm"], 1)

            def output(e, j, par, first=False):
                U, r = e * NU + j, j % 2
                if j == 0 and not first:
                    pe.wait_ge(s["added"], e * NB - (NB - 1))
                pe.wait_ge(s["w2_lo"], U + 1)
                pe.wait_ge(s["h_lo"], U + 3)
                for b in range(NB):
                    for n in range(NP):
                        ins = split_matmul(pe, y_ps[:, par, b, :], h_hi[:, r, n, b * P:(b + 1) * P],
                                           h_lo[:, r, n, b * P:(b + 1) * P], w2_hi[:, r, n, :], w2_lo[:, r, n, :],
                                           j == 0 and n == 0, j == NU - 1 and n == NP - 1)
                ins.then_inc(s["y_mm"], 1)
            hidden(0, 0, first=True)

            def expert(e, par, first=False, last=False):
                for j in range(NU):
                    if not (last and j == NU - 1):
                        hidden(e, j + 1, first and j == 0)
                    output(e, j, par, first)
            expert(0, 0, first=True)
            with pe.Fori(0, E // 2 - 1) as i:
                for half in range(2):
                    expert(i * 2 + half + 1, 1 - half)
            expert(E - 1, 1, last=True)


STOP = 9


def kernel(**inputs):
    import numpy as np
    import concourse.bacc as bacc
    from concourse.bass_utils import run_bass_kernel_spmd

    x = {k: np.asarray(v) for k, v in inputs.items()}
    cols = lambda a: a.reshape(-1, 4, 128).transpose(0, 2, 1).reshape(-1, 128, 4)
    sign = np.repeat(np.array([0.125, 0.125, 0.125, -0.125], np.float32), 32)[:, None]
    vecs = np.concatenate([cols(x["L0_xattn_" + n])[0] for n in ("ln_lat_g", "ln_lat_b", "ln_ctx_g", "ln_ctx_b")]
                          + [sign], axis=1)
    wq = x["L0_xattn_Wq"].reshape(512, 16, 2, 32)[:, :, [0, 1, 1, 0], :].reshape(512, 2048)

    def quads(w):
        return w.reshape(4, 128, 4, 256).transpose(2, 1, 0, 3).reshape(4 * 128, 1024)

    wk, wv = quads(x["L0_xattn_Wkv"][:, :1024]), quads(x["L0_xattn_Wkv"][:, 1024:])
    theta = 1.0 / np.float32(10000.0) ** (np.float32(2.0) * np.arange(16, dtype=np.float32) / np.float32(32))
    angle = np.arange(128, dtype=np.float32)[:, None] * theta[None, :].astype(np.float32)
    rope = np.cos(angle).astype(np.float32), np.sin(angle).astype(np.float32)
    arrays = {
        "x": x["x"], "ident": np.eye(128, dtype=np.float32), "vecs": vecs, "wq_stack": wq,
        "cos_T4": np.tile(x["L0_xattn_cos"].T, (4, 1)), "sin_T4": np.tile(x["L0_xattn_sin"].T, (4, 1)),
        "ctx_rows": x["ctx_1024"].reshape(4096, 512),
        "wk_rows": wk, "wv_rows": np.concatenate([wv, wv[:128]]), "wo0": x["L0_xattn_Wo"],
        "bo0": x["L0_xattn_bo"][None],
        "causal4": np.tile(np.where(np.tril(np.ones((128, 128), bool)), 0, MASKED).astype(np.float32), (1, 4)),
        "sa0_wq": x["L0_attn_wq"].T, "sa0_wk": x["L0_attn_wk"].T, "sa0_wv": x["L0_attn_wv"].T,
        "sa0_wp": x["L0_attn_wp"].T,
        "sa0_rows": np.concatenate([x["L0_attn_b" + n] for n in "qkvp"])[None],
        "sa0_rc": np.tile(rope[0], (1, 32)), "sa0_rs": np.tile(rope[1], (1, 32)),
        "sgn_w": x["L0_ffn_weight"].T,
        "mask": x["mask_Bx1xSxS2_ff0"].reshape(2, 128, 2048),
        "ctx_T": x["ctx_1024"].transpose(0, 2, 1).reshape(1024, 2048),
        "ctx_heads": x["ctx_1024"].reshape(2, 16, 128, 4, 128).transpose(0, 3, 2, 1, 4).reshape(1024, 2048),
        "wo1": x["L1_xattn_wo_w"].T, "wo1_row": x["L1_xattn_wo_b"][None],
        "sa1_wq": x["L1_attn_query_mat"].reshape(512, 1024), "sa1_wk": x["L1_attn_key_mat"].reshape(512, 1024),
        "sa1_wv": x["L1_attn_value_mat"].reshape(512, 1024), "sa1_wp": x["L1_attn_linear_m1"],
        "w1": x["L1_ffn_W1"].reshape(8, 4, 128, 4, 512).transpose(0, 3, 2, 1, 4).reshape(4096, 2048),
        "w2": x["L1_ffn_W2"].reshape(8, 4, 4, 128, 512).transpose(0, 1, 3, 2, 4).reshape(4096, 2048),
        "b1": x["L1_ffn_b1"].reshape(128, 128).T, "b2": x["L1_ffn_b2"],
        "wr": x["L1_ffn_Wr"].reshape(4, 128, 8).transpose(1, 0, 2), "br": x["L1_ffn_br"][None],
        "before": np.tile(np.tril(np.ones((8, 8), np.float32), -1).reshape(1, 64), (128, 1)),
    }
    nc = bacc.Bacc("TRN2", target_bir_lowering=False, num_devices=1)
    aps, named = {}, {}
    for name, a in arrays.items():
        a = np.ascontiguousarray(a)
        named["in_" + name] = a
        aps[name] = nc.dram_tensor("in_" + name, a.shape, mybir.dt.from_np(a.dtype), kind="ExternalInput").ap()
    aps["wv_quads"] = aps["wv_rows"].rearrange("(g p) n -> g p n", p=128)
    out = nc.dram_tensor("out_x", (2, 128, 512), F32, kind="ExternalOutput").ap()
    program(nc, aps, out)
    r = run_bass_kernel_spmd(nc, [named], core_ids=[0])
    return r.results[0]["out_x"]
```

```python
from contextlib import ExitStack

import concourse.bass as bass
from concourse import mybir

F32 = mybir.dt.float32
F32R = mybir.dt.float32r
ACT = mybir.ActivationFunctionType
ALU = mybir.AluOpType
AX = mybir.AxisListType

P = 128
NB = 2
D = 512
KD = D // P
S = 2048
NCH = S // P
NG = S // 512
TOK = NB * P
EPS = 1e-5

H = 16
DH0 = 64
DHS = 32
NQ = 4
E_MOE = 8
F_MOE = 2048
NU = F_MOE // 512
MASKED = -1e30

LO_CLIP = 1.670170079024566e-05
HI_CLIP = 59874.14171519782


class Chain:

    def __init__(self, eng, sem, start=0):
        self.eng, self.sem, self.n = eng, sem, start

    def __call__(self, ins):
        self.n += 1
        ins.then_inc(self.sem, 1)
        self.eng.wait_ge(self.sem, self.n)


def split_matmul(pe, out, w_hi, w_lo, x_hi, x_lo, start, stop):
    pe.matmul(out, w_hi, x_hi, start=start, stop=False)
    pe.matmul(out, w_hi, x_lo, start=False, stop=False)
    return pe.matmul(out, w_lo, x_hi, start=False, stop=stop)


def program(nc, I, out):
    top = ExitStack()
    with top:
        def sem(name):
            return top.enter_context(nc.semaphore(name))

        def sb_in(stack, name, shape, dt=F32):
            return stack.enter_context(nc.sbuf_tensor(name, shape, dt))

        def ps_in(stack, name, shape):
            return stack.enter_context(nc.psum_tensor(name, shape, F32))

        resid = sb_in(top, "resid", [P, NB, D])
        ident = sb_in(top, "ident", [P, P])
        ones_row = sb_in(top, "ones_row", [1, P])
        normed = sb_in(top, "normed", [P, NB, D])
        normed_T = sb_in(top, "normed_T", [P, KD, TOK])
        ln_stats = sb_in(top, "ln_stats", [P, NB, 6])
        ln_mv = sb_in(top, "ln_mv", [P, NB, 2])
        ln_var = sb_in(top, "ln_var", [P, NB])
        ln_std = sb_in(top, "ln_std", [P, NB])
        ln_rstd = sb_in(top, "ln_rstd", [P, NB])

        consts_in = sem("consts_in")
        ones_set = sem("ones_set")

        dve_step, var_ready, std_ready, ln_ready, T_ready, T_done = (
            sem(f"ln_{n}") for n in ("dve_step", "var_ready", "std_ready", "ln_ready", "T_ready", "T_done"))
        ln_count = {"step": 0, "var": 0, "ln": 0, "T": 0}

        def layer_norm_T(tag, times=1, scale_bias=None, first_wait=None):
            step0, var0, ln0, T0 = (ln_count[n] for n in ("step", "var", "ln", "T"))
            ln_count["step"] += 7 * times - 2 if times > 1 else 5
            ln_count["var"] += times
            ln_count["ln"] += NB
            ln_count["T"] += 2
            with ExitStack() as st:
                T_ps = ps_in(st, f"{tag}_T_ps", [P, KD, TOK])
                block = st.enter_context(nc.Block())

                @block.vector
                def _(dve):
                    if first_wait:
                        dve.wait_ge(*first_wait)
                    step = Chain(dve, dve_step, step0)
                    for t in range(times):
                        src = resid if t == 0 else normed
                        for b in range(NB):
                            step(dve.bn_stats(ln_stats[:, b, :], src[:, b, :]))
                        for b in range(NB):
                            step(dve.bn_aggr(ln_mv[:, b, :], ln_stats[:, b, :]))
                        dve.tensor_scalar(ln_var[:], ln_mv[:, :, 1], EPS, None, ALU.add).then_inc(var_ready, 1)
                        dve.wait_ge(std_ready, var0 + t + 1)
                        step(dve.reciprocal(ln_rstd[:], ln_std[:]))
                        for b in range(NB):
                            ins = dve.tensor_scalar(normed[:, b, :], src[:, b, :], ln_mv[:, b, 0:1],
                                                    ln_rstd[:, b:b + 1], ALU.subtract, ALU.mult)
                            if t < times - 1:
                                step(ins)
                            else:
                                ins.then_inc(ln_ready, 1)

                @block.scalar
                def _(act):
                    for t in range(times):
                        act.wait_ge(var_ready, var0 + t + 1)
                        act.activation(ln_std[:], ln_var[:], ACT.Sqrt).then_inc(std_ready, 1)
                    if scale_bias is None:
                        for half in range(2):
                            act.wait_ge(T_ready, T0 + half + 1)
                            act.activation(normed_T[:, 2 * half:2 * half + 2, :], T_ps[:, 2 * half:2 * half + 2, :],
                                           ACT.Copy).then_inc(T_done, 1)
                    else:
                        g_col, b_col = scale_bias
                        for k in range(KD):
                            act.wait_ge(T_ready, T0 + k // 2 + 1)
                            act.activation(normed_T[:, k, :], T_ps[:, k, :], ACT.Identity,
                                           bias=b_col[:, k:k + 1], scale=g_col[:, k:k + 1]).then_inc(T_done, 1)

                @block.tensor
                def _(pe):
                    pe.wait_ge(ln_ready, ln0 + NB)
                    if first_wait:
                        pe.wait_ge(*first_wait)
                    for k in range(KD):
                        for b in range(NB):
                            ins = pe.transpose(T_ps[:, k, b * P:(b + 1) * P], normed[:, b, k * P:(k + 1) * P],
                                               ident[:])
                        if k % 2:
                            ins.then_inc(T_ready, 1)

        with nc.Block() as block:
            @block.sync
            def _(sp):
                for b in range(NB):
                    sp.dma_start(resid[:, b, :], I["x"][b]).then_inc(consts_in, 16)
                sp.dma_start(ident[:], I["ident"]).then_inc(consts_in, 16)

            @block.vector
            def _(dve):
                dve.memset(ones_row[:], 1.0).then_inc(ones_set, 1)

        cross_attention_rotary(nc, I, locals())
        with ExitStack() as after:
            behind_cross_attention(nc, I, locals(), after)

        stored = sem("stored")
        with nc.Block() as block:
            @block.sync
            def _(sp):
                for b in range(NB):
                    sp.dma_start(out[b], resid[:, b, :]).then_inc(stored, 16)
                sp.wait_ge(stored, 16 * NB)


def behind_cross_attention(nc, I, env, outer):
    sem, sb_in = env["sem"], env["sb_in"]

    def load_block(name, loads):
        got = sem(name)
        with nc.Block() as block:
            @block.sync
            def _(sp):
                for dst, src in loads:
                    sp.dma_start(dst, src).then_inc(got, 16)
        return got

    rows4 = lambda n: I[n].rearrange("(k p) n -> p k n", p=P)
    env["sa1_w"] = [sb_in(outer, f"sa1_{n}", [P, KD, 1024]) for n in ("wq", "wk", "wv")]
    env["sa1_wq"], env["sa1_wk"], env["sa1_wv"] = env["sa1_w"]
    causal = sb_in(outer, "causal", [P, D])
    env["sa0_mask"] = env["sa1_mask"] = causal
    env["sa1_rows"] = env["sa1_rc"] = env["sa1_rs"] = None
    with ExitStack() as st:
        loads = [(causal[:], I["causal4"])]
        for n in ("wq", "wk", "wv", "wp"):
            env["sa0_" + n] = sb_in(st, "sa0_" + n, [P, KD, D])
        env["sa0_rows"] = sb_in(st, "sa0_rows", [1, 4 * D])
        for n in ("rc", "rs"):
            env["sa0_" + n] = sb_in(st, "sa0_" + n, [P, D])
        sgn_w = sb_in(st, "sgn_w", [P, KD, D])
        loads += [(env["sa0_" + n][:], rows4("sa0_" + n)) for n in ("wq", "wk", "wv")]
        loads += [(env["sa0_rows"][:], I["sa0_rows"]), (env["sa0_rc"][:], I["sa0_rc"]),
                  (env["sa0_rs"][:], I["sa0_rs"]), (env["sa0_wp"][:], rows4("sa0_wp"))]
        env["sa0_w_in"], env["sa0_w_count"] = load_block("sa0_w_in", loads), len(loads)
        env["sgn_w"], env["sgn_w_need"] = sgn_w, 16
        env["sgn_w_in"] = load_block("sgn_w_in", [(sgn_w[:], rows4("sgn_w"))])
        env["sa0_wp_in"] = (env["sa0_w_in"], 16 * env["sa0_w_count"])
        env["sa1_w_in"], env["sa1_w_count"] = load_block(
            "sa1_w_in", [(t[:], rows4(n)) for t, n in zip(env["sa1_w"], ("sa1_wq", "sa1_wk", "sa1_wv"))]), 3
        self_attention(nc, I, env, "sa0", DHS, 0)
        if STOP >= 3:
            sign_layer(nc, I, env)
    if STOP >= 4:
        with ExitStack() as st:
            env["wo1"] = sb_in(st, "wo1", [P, KD, D])
            env["wo1_row"] = sb_in(st, "wo1_row", [1, D])
            cross_attention_masked(nc, I, env)
    if STOP >= 5:
        w1_raw = env["w1_raw"] = sb_in(outer, "w1_raw", [P, 2, KD, 512])
        w2_raw = env["w2_raw"] = sb_in(outer, "w2_raw", [P, 2, 4, D])
        env["w1_in"], env["w2_in"] = ([sem(f"{n}_in{r}") for r in range(2)] for n in ("w1", "w2"))
        with ExitStack() as st:
            wp = env["sa1_wp"] = sb_in(st, "sa1_wp", [P, 8, D])
            env["sa1_wp_in"] = (load_block("sa1_wp_in", [(wp[:], rows4("sa1_wp"))]), 16)
            with nc.Block() as block:
                @block.sync
                def _(sp):
                    for U in range(2):
                        for raw, name, got in ((w1_raw, "w1", env["w1_in"]), (w2_raw, "w2", env["w2_in"])):
                            sp.dma_start(raw[:, U, :, :], I[name][U * P:(U + 1) * P, :]
                                         .rearrange("p (k n) -> p k n", k=4)).then_inc(got[U], 16)
            self_attention(nc, I, env, "sa1", DH0, 1)
    if STOP >= 6:
        experts(nc, I, env)


def cross_attention_rotary(nc, I, env):
    sem, sb_in, ps_in = env["sem"], env["sb_in"], env["ps_in"]
    resid, ident, ones_row, normed_T = env["resid"], env["ident"], env["ones_row"], env["normed_T"]
    consts_in = env["consts_in"]

    outer = ExitStack()
    with outer:
        q_stack = sb_in(outer, "q_stack", [P, NB * H * P])
        attn = sb_in(outer, "attn", [P, NB * H * DH0])
        vecs = sb_in(outer, "vecs", [P, 4 * KD + 1])
        lat_g, lat_b = vecs[:, 0:KD], vecs[:, KD:2 * KD]
        ctx_g, ctx_b = vecs[:, 2 * KD:3 * KD], vecs[:, 3 * KD:4 * KD]
        q_sign = vecs[:, 4 * KD:4 * KD + 1]

        q_ready, q_done, vecs_in = (sem(n) for n in ("q_ready", "q_done", "vecs_in"))
        wq_in = [sem(f"wq_in{n}") for n in range(4)]
        names = ("tab_in", "ctx_in0", "ctx_in1", "ctx_free", "cvar", "cstd", "ctp", "cfull", "csplit",
                 "cstep", "wv_in", "wk_in", "wk_hi_done", "wk_lo_done", "wv_hi_done", "wv_lo_done",
                 "v_mm", "v_out", "k_mm", "rope_done", "sc_done", "exp_done", "clip_done", "pv_done",
                 "norm_done", "qcur_done", "vones", "den_step", "norm_step")
        s = {n: sem("x0_" + n) for n in names}
        ctx_raw = sb_in(outer, "ctx_raw", [P, 2, 4, D])
        cst = sb_in(outer, "cst", [P, 2, 4, 6])
        cmv = sb_in(outer, "cmv", [P, 2, 4, 2])
        cva = sb_in(outer, "cva", [P, 2, 4])
        csd = sb_in(outer, "csd", [P, 2, 4])
        crs = sb_in(outer, "crs", [P, 2, 4])
        wv_raw = sb_in(outer, "wv_raw", [P, KD, 256])
        bo = sb_in(outer, "bo", [1, D])
        wo = ctx_raw[:].rearrange("p a c d -> p (a c) d")
        wo_in = sem("x0o_wo_in")

        def load_context(sp, b, grp):
            sp.dma_start(ctx_raw[:, grp % 2, :, :],
                         I["ctx_rows"][b * S + grp * 512:b * S + (grp + 1) * 512, :]
                         .rearrange("(c p) d -> p c d", p=P)).then_inc(s[f"ctx_in{grp % 2}"], 16)

        def center(dve, b, grp):
            r = grp % 2
            base = b * 52 + grp * 13
            dve.wait_ge(s[f"ctx_in{r}"], b * 32 + 16 * (grp // 2 + 1))
            for c in range(4):
                dve.bn_stats(cst[:, r, c, :], ctx_raw[:, r, c, :]).then_inc(s["cstep"], 1)
            dve.wait_ge(s["cstep"], base + 4)
            for c in range(4):
                dve.bn_aggr(cmv[:, r, c, :], cst[:, r, c, :]).then_inc(s["cstep"], 1)
            dve.wait_ge(s["cstep"], base + 8)
            dve.tensor_scalar(cva[:, r, :], cmv[:, r, :, 1], EPS, None, ALU.add).then_inc(s["cvar"], 1)
            dve.wait_ge(s["cstd"], b * NG + (grp + 1))
            dve.reciprocal(crs[:, r, :], csd[:, r, :]).then_inc(s["cstep"], 1)
            dve.wait_ge(s["cstep"], base + 9)
            for c in range(4):
                dve.tensor_scalar(ctx_raw[:, r, c, :], ctx_raw[:, r, c, :], cmv[:, r, c, 0:1],
                                  crs[:, r, c:c + 1], ALU.subtract, ALU.mult).then_inc(s["cstep"], 1)

        def root(act, b, grp):
            act.wait_ge(s["cvar"], b * NG + (grp + 1))
            act.activation(csd[:, grp % 2, :], cva[:, grp % 2, :], ACT.Sqrt).then_inc(s["cstd"], 1)

        with ExitStack() as st:
            wq = sb_in(st, "wq_stack", [P, KD, H * P])
            with nc.Block() as block:
                @block.sync
                def _(sp):
                    sp.dma_start(vecs[:], I["vecs"]).then_inc(vecs_in, 16)
                    for n in range(4):
                        sp.dma_start(wq[:, :, n * 512:(n + 1) * 512], I["wq_stack"][:, n * 512:(n + 1) * 512]
                                     .rearrange("(k p) n -> p k n", p=P)).then_inc(wq_in[n], 16)
                    for grp in range(2):
                        load_context(sp, 0, grp)
                    sp.dma_start(wv_raw[:], I["wv_quads"][0].rearrange("p (k n) -> p k n", k=KD))\
                        .then_inc(s["wv_in"], 16)

                @block.scalar
                def _(act):
                    act.wait_ge(vecs_in, 16)
            env["layer_norm_T"]("ln0", times=2, scale_bias=(lat_g, lat_b), first_wait=(consts_in, 48))
            q_ps = ps_in(st, "q_ps", [P, 4, 2, TOK])
            block = st.enter_context(nc.Block())

            @block.tensor
            def _(pe):
                for h in range(H):
                    n = h // 2
                    if h % 4 == 0:
                        pe.wait_ge(wq_in[h // 4], 16)
                    if h % 2 == 0 and n >= 4:
                        pe.wait_ge(q_done, n - 3)
                    for k in range(KD):
                        ins = pe.matmul(q_ps[:, n % 4, h % 2, :], wq[:, k, h * P:(h + 1) * P], normed_T[:, k, :],
                                        start=(k == 0), stop=(k == KD - 1))
                    if h % 2:
                        ins.then_inc(q_ready, 1)

            @block.scalar
            def _(act):
                q_view = q_stack[:].rearrange("p (b h t) -> p h b t", b=NB, h=H)
                for n in range(H // 2):
                    if n >= H // 2 - 2:
                        root(act, 0, n - (H // 2 - 2))
                    act.wait_ge(q_ready, n + 1)
                    act.activation(q_view[:, 2 * n:2 * n + 2, :, :],
                                   q_ps[:, n % 4, :, :].rearrange("p h (b t) -> p h b t", b=NB), ACT.Copy,
                                   scale=q_sign).then_inc(q_done, 1)

            @block.vector
            def _(dve):
                for grp in range(2):
                    center(dve, 0, grp)

        with ExitStack() as st:
            cos_T = sb_in(st, "cos_T", [P, S])
            sin_T = sb_in(st, "sin_T", [P, S])
            ctx_hi = sb_in(st, "ctx_hi", [P, KD, S], F32R)
            ctx_lo = sb_in(st, "ctx_lo", [P, KD, S], F32R)
            wv_hi = sb_in(st, "wv_hi", [P, KD, 256], F32R)
            wv_lo = sb_in(st, "wv_lo", [P, KD, 256], F32R)
            wk_raw = sb_in(st, "wk_raw", [P, KD, 256])
            wk_hi = sb_in(st, "wk_hi", [P, KD, 256], F32R)
            wk_lo = sb_in(st, "wk_lo", [P, KD, 256], F32R)
            vals = sb_in(st, "vals", [P, NCH, 4, DH0 + 1])
            keys = sb_in(st, "keys", [P, 3, 2, 512])
            prob = sb_in(st, "prob", [P, 3, 2, 512])
            ctx_full = prob[:, 0:2, :, :].rearrange("p a b n -> p (a b) n")
            q_cur = sb_in(st, "q_cur", [P, 4 * P])
            rden = sb_in(st, "rden", [P, 4])
            k_ps = ps_in(st, "k_ps", [P, 2, 512])
            u_ps = ps_in(st, "u_ps", [P, 4, 512])
            o_ps = ps_in(st, "o_ps", [P, 2, 512])
            block = st.enter_context(nc.Block())

            @block.sync
            def _(sp):
                for b in range(NB):
                    for grp in range(2 if b == 0 else 0, NG):
                        sp.wait_ge(s["ctx_free"], b * NG + (grp - 1))
                        load_context(sp, b, grp)
                    if b == NB - 1:
                        sp.wait_ge(s["ctx_free"], NB * NG)
                        sp.dma_start(wo, I["wo0"].rearrange("(k p) n -> p k n", p=P)).then_inc(wo_in, 16)
                        sp.dma_start(bo[:], I["bo0"]).then_inc(wo_in, 16)
                    with sp.Fori(0, NQ) as g:
                        u = b * NQ + g
                        sp.wait_ge(s["wk_lo_done"], u + 1)
                        sp.dma_start(wk_raw[:], I["wk_rows"][bass.ds(g * P, P), :]
                                     .rearrange("p (k n) -> p k n", k=KD)).then_inc(s["wk_in"], 16)
                        sp.wait_ge(s["wv_lo_done"], u + 1)
                        sp.dma_start(wv_raw[:], I["wv_rows"][bass.ds(g * P + P, P), :]
                                     .rearrange("p (k n) -> p k n", k=KD)).then_inc(s["wv_in"], 16)

            @block.gpsimd
            def _(pool):
                pool.dma_start(cos_T[:], I["cos_T4"]).then_inc(s["tab_in"], 16)
                pool.dma_start(sin_T[:], I["sin_T4"]).then_inc(s["tab_in"], 16)
                pool.memset(vals[:, :, :, DH0:DH0 + 1], 1.0).then_inc(s["vones"], 1)
                for b in range(NB):
                    for grp in range(NG):
                        cols = slice(grp * 512, (grp + 1) * 512)
                        for k in range(KD):
                            pool.wait_ge(s["cfull"], b * 16 + (grp * KD + k + 1))
                            pool.tensor_tensor(ctx_lo[:, k, cols], ctx_full[:, k, :], ctx_hi[:, k, cols],
                                               ALU.subtract).then_inc(s["csplit"], 1)

            @block.vector
            def _(dve):
                dve.sem_inc(s["wk_lo_done"], 1)
                dve.wait_ge(s["wv_hi_done"], 1)
                dve.tensor_tensor(wv_lo[:], wv_raw[:], wv_hi[:], ALU.subtract).then_inc(s["wv_lo_done"], 1)
                for b in range(NB):
                    if b > 0:
                        center(dve, b, 0)
                        center(dve, b, 1)
                    for grp in range(2, NG):
                        center(dve, b, grp)
                    if b == 0:
                        dve.wait_ge(s["tab_in"], 32)
                    with dve.Fori(0, NQ) as g:
                        u = b * NQ + g
                        dve.wait_ge(s["sc_done"], u * 16 + 1)
                        dve.tensor_copy(q_cur[:], q_stack[:, bass.ds(u * (4 * P), 4 * P)]).then_inc(s["qcur_done"], 1)
                        dve.wait_ge(s["wk_hi_done"], u + 1)
                        dve.tensor_tensor(wk_lo[:], wk_raw[:], wk_hi[:], ALU.subtract).then_inc(s["wk_lo_done"], 1)

                        def rope(n):
                            c = n % 4
                            dve.wait_ge(s["k_mm"], u * 8 + (n + 2))
                            if n >= 3:
                                dve.wait_ge(s["sc_done"], u * 16 + (2 * (n - 2) + 1))
                            for hh in range(2):
                                rows = slice(hh * 64, hh * 64 + 64)
                                for t, tab in enumerate((cos_T, sin_T)):
                                    dve.tensor_tensor(keys[64 * t:64 * t + 64, n % 3, hh, :], k_ps[rows, n % 2, :],
                                                      tab[rows, c * 512:(c + 1) * 512],
                                                      ALU.mult).then_inc(s["rope_done"], 1)

                        def clip(n):
                            for hh in range(2):
                                dve.wait_ge(s["exp_done"], u * 16 + (2 * n + hh + 1))
                                dve.tensor_scalar(prob[:, n % 3, hh, :], prob[:, n % 3, hh, :], LO_CLIP, HI_CLIP,
                                                  ALU.max, ALU.min).then_inc(s["clip_done"], 1)

                        def normalise(pr):
                            for hh in range(2):
                                i = 2 * pr + hh
                                dve.wait_ge(s["pv_done"], u * 16 + (2 * (4 * pr + 3) + hh + 2))
                                dve.reciprocal(rden[:, i:i + 1], o_ps[:, hh, DH0:DH0 + 1]).then_inc(s["den_step"], 1)
                                dve.wait_ge(s["den_step"], u * 4 + (i + 1))
                                dve.tensor_scalar(attn[:, bass.ds(u * (4 * DH0) + i * DH0, DH0)],
                                                  o_ps[:, hh, 0:DH0], rden[:, i:i + 1], None,
                                                  ALU.mult).then_inc(s["norm_done"], 1)
                        for n in range(8):
                            if n == 6:
                                normalise(0)
                            rope(n)
                            if n >= 1:
                                clip(n - 1)
                            if n == 4:
                                dve.wait_ge(s["wv_hi_done"], u + 2)
                                dve.tensor_tensor(wv_lo[:], wv_raw[:], wv_hi[:],
                                                  ALU.subtract).then_inc(s["wv_lo_done"], 1)
                        clip(7)
                        normalise(1)

            @block.scalar
            def _(act):
                act.wait_ge(s["wv_in"], 16)
                act.activation(wv_hi[:], wv_raw[:], ACT.Copy).then_inc(s["wv_hi_done"], 1)
                for b in range(NB):
                    if b > 0:
                        root(act, b, 0)
                        root(act, b, 1)
                    for grp in range(NG):
                        if grp >= 2:
                            root(act, b, grp)
                        for k in range(KD):
                            n = grp * KD + k
                            act.wait_ge(s["ctp"], b * 16 + (n + 1))
                            if n >= 4:
                                act.wait_ge(s["csplit"], b * 16 + (n - 3))
                            for dst in (ctx_full[:, k, :], ctx_hi[:, k, grp * 512:(grp + 1) * 512]):
                                ins = act.activation(dst, u_ps[:, k, :], ACT.Identity, bias=ctx_b[:, k:k + 1],
                                                     scale=ctx_g[:, k:k + 1])
                            ins.then_inc(s["cfull"], 1)
                    with act.Fori(0, NQ) as g:
                        u = b * NQ + g
                        act.wait_ge(s["wk_in"], u * 16 + 16)
                        act.wait_ge(s["k_mm"], u * 8 + 1)
                        act.activation(wk_hi[:], wk_raw[:], ACT.Copy).then_inc(s["wk_hi_done"], 1)
                        for i in range(8):
                            act.wait_ge(s["v_mm"], u * 8 + (i + 1))
                            act.activation(vals[:, 2 * i:2 * i + 2, :, 0:DH0],
                                           u_ps[:, i % 4, :].rearrange("p (c h d) -> p c h d", c=2, h=4),
                                           ACT.Copy).then_inc(s["v_out"], 1)
                        for n in range(8):
                            for hh in range(2):
                                w = 2 * n + hh
                                act.wait_ge(s["sc_done"], u * 16 + (w + 2))
                                act.wait_ge(s["pv_done"], u * 16 + (max(w - 6 + 1, 0) + 1))
                                act.activation(prob[:, n % 3, hh, :], u_ps[:, w % 4, :],
                                               ACT.Exp).then_inc(s["exp_done"], 1)
                            if n == 2:
                                act.wait_ge(s["wv_in"], u * 16 + 32)
                                act.activation(wv_hi[:], wv_raw[:], ACT.Copy).then_inc(s["wv_hi_done"], 1)

            @block.tensor
            def _(pe):
                for n in ("sc_done", "pv_done", "k_mm", "norm_done"):
                    pe.sem_inc(s[n], 1)
                pe.wait_ge(s["vones"], 1)
                for b in range(NB):
                    for grp in range(NG):
                        pe.wait_ge(s["cstep"], b * 52 + (grp * 13 + 13))
                        for k in range(KD):
                            n = grp * KD + k
                            if n >= 4:
                                pe.wait_ge(s["cfull"], b * 16 + (n - 3))
                            for c in range(4):
                                ins = pe.transpose(u_ps[:, k, c * P:(c + 1) * P],
                                                   ctx_raw[:, grp % 2, c, k * P:(k + 1) * P], ident[:])
                            ins.then_inc(s["ctp"], 1)
                        pe.wait_ge(s["cfull"], b * 16 + (grp * KD + KD))
                        pe.sem_inc(s["ctx_free"], 1)

                    with pe.Fori(0, NQ) as g:
                        u = b * NQ + g
                        pe.wait_ge(s["csplit"], b * 16 + 16)
                        pe.wait_ge(s["wv_lo_done"], u + 1)
                        for i in range(8):
                            if i >= 4:
                                pe.wait_ge(s["v_out"], u * 8 + (i - 3))
                            for c in range(2):
                                rows = slice((2 * i + c) * P, (2 * i + c + 1) * P)
                                for k in range(KD):
                                    ins = split_matmul(pe, u_ps[:, i % 4, c * 256:(c + 1) * 256],
                                                       ctx_hi[:, k, rows], ctx_lo[:, k, rows],
                                                       wv_hi[:, k, :], wv_lo[:, k, :], k == 0, k == KD - 1)
                            ins.then_inc(s["v_mm"], 1)

                        def project(n):
                            pr, c = n // 4, n % 4
                            if n == 0:
                                pe.wait_ge(s["wk_lo_done"], u + 2)
                            if n >= 2:
                                pe.wait_ge(s["rope_done"], u * 32 + 4 * (n - 1))
                            for k in range(KD):
                                ins = split_matmul(pe, k_ps[:, n % 2, :], wk_hi[:, k, pr * P:(pr + 1) * P],
                                                   wk_lo[:, k, pr * P:(pr + 1) * P],
                                                   ctx_hi[:, k, c * 512:(c + 1) * 512],
                                                   ctx_lo[:, k, c * 512:(c + 1) * 512], k == 0, k == KD - 1)
                            ins.then_inc(s["k_mm"], 1)

                        def scores(n):
                            pr = n // 4
                            if n == 0:
                                pe.wait_ge(s["v_out"], u * 8 + 8)
                                pe.wait_ge(s["qcur_done"], u + 1)
                            pe.wait_ge(s["rope_done"], u * 32 + 4 * (n + 1))
                            for hh in range(2):
                                w = 2 * n + hh
                                if w >= 4:
                                    pe.wait_ge(s["exp_done"], u * 16 + (w - 3))
                                hd = 2 * pr + hh
                                for j in range(4):
                                    ins = pe.matmul(u_ps[:, w % 4, j * P:(j + 1) * P],
                                                    keys[:, n % 3, hh, j * P:(j + 1) * P],
                                                    q_cur[:, hd * P:(hd + 1) * P], start=True, stop=True)
                                ins.then_inc(s["sc_done"], 1)

                        def weigh(n):
                            pr, c = n // 4, n % 4
                            if c == 0:
                                pe.wait_ge(s["norm_done"], u * 4 + (2 * pr + 1))
                            for hh in range(2):
                                pe.wait_ge(s["clip_done"], u * 16 + (2 * n + hh + 1))
                                for j in range(4):
                                    ins = pe.matmul(o_ps[:, hh, 0:DH0 + 1], prob[:, n % 3, hh, j * P:(j + 1) * P],
                                                    vals[:, 4 * c + j, 2 * pr + hh, :],
                                                    start=(c == 0 and j == 0), stop=(c == 3 and j == 3))
                                ins.then_inc(s["pv_done"], 1)
                        for n in range(10):
                            if n < 8:
                                project(n)
                            if 1 <= n <= 8:
                                scores(n - 1)
                            if n >= 2:
                                weigh(n - 2)

        aT_ready, aT_done, y_ready, r_done = (sem("x0o_" + n) for n in ("aT_ready", "aT_done", "y_ready", "r_done"))
        with ExitStack() as st:
            attn_T = sb_in(st, "attn_T", [P, 8, TOK])
            a_ps = ps_in(st, "a_ps", [P, 4, 2, TOK])
            y_ps = ps_in(st, "y_ps", [P, NB, D])
            block = st.enter_context(nc.Block())

            @block.tensor
            def _(pe):
                for j in range(4):
                    for c in range(2):
                        for b in range(NB):
                            k = 2 * j + c
                            ins = pe.transpose(a_ps[:, j, c, b * P:(b + 1) * P],
                                               attn[:, b * 1024 + k * P:b * 1024 + (k + 1) * P], ident[:])
                    ins.then_inc(aT_ready, 1)
                pe.wait_ge(wo_in, 32)
                for b in range(NB):
                    pe.matmul(y_ps[:, b, :], ones_row[:], bo[:], start=True, stop=False)
                    for k in range(8):
                        if b == 0 and k % 2 == 0:
                            pe.wait_ge(aT_done, k // 2 + 1)
                        ins = pe.matmul(y_ps[:, b, :], attn_T[:, k, b * P:(b + 1) * P], wo[:, k, :],
                                        start=False, stop=(k == 7))
                    ins.then_inc(y_ready, 1)

            @block.scalar
            def _(act):
                for j in range(4):
                    act.wait_ge(aT_ready, j + 1)
                    act.activation(attn_T[:, 2 * j:2 * j + 2, :], a_ps[:, j, :, :], ACT.Copy).then_inc(aT_done, 1)

            @block.vector
            def _(dve):
                for b in range(NB):
                    dve.wait_ge(y_ready, b + 1)
                    dve.tensor_tensor(resid[:, b, :], y_ps[:, b, :], resid[:, b, :], ALU.add).then_inc(r_done, 1)


def self_attention(nc, I, env, tag, dh, layer):
    sem, sb_in, ps_in = env["sem"], env["sb_in"], env["ps_in"]
    resid, ident, ones_row, normed_T = env["resid"], env["ident"], env["ones_row"], env["normed_T"]
    per = P // dh
    KA = H // per
    W = H * dh
    NW = W // D
    scale = dh ** -0.5 if layer == 0 else dh ** 0.5
    wq, wk, wv, wp, rows, rope_c, rope_s, mask = (env[f"{tag}_{n}"] for n in
                                                  ("wq", "wk", "wv", "wp", "rows", "rc", "rs", "mask"))
    w_in, w_count = env[f"{tag}_w_in"], env[f"{tag}_w_count"]
    s = {n: sem(f"{tag}_{n}") for n in
         ("proj", "qk_out", "v_out", "rope", "qkT", "qkT_out", "score", "masked", "maxed", "shifted", "exped",
          "den", "pT", "pT_out", "pv", "normed", "aT", "aT_out", "y", "done")}

    env["layer_norm_T"](tag + "ln")
    with ExitStack() as st:
        qT = sb_in(st, tag + "qT", [P, KA, TOK])
        kT = sb_in(st, tag + "kT", [P, KA, TOK])
        v = sb_in(st, tag + "v", [P, NB, W])
        if layer == 0:
            turned = sb_in(st, tag + "turned", [P, NB, 2, D])
            part = sb_in(st, tag + "part", [P, NB, 4, 2, D // 2])
        sc = sb_in(st, tag + "sc", [P, NB, H * P])
        pT = sb_in(st, tag + "pT", [P, NB, H * P])
        stat = sb_in(st, tag + "stat", [P, 3, NB, H])
        attn = sb_in(st, tag + "attn", [P, NB, W])
        attn_T = sb_in(st, tag + "attn_T", [P, KA, TOK])
        bk = [ps_in(st, f"{tag}bk{b}", [P, 4, D]) for b in range(NB)]
        block = st.enter_context(nc.Block())

        def place(h):
            n = (h % per) * (H // per) + h // per
            return n // 4, (n % 4) * P

        @block.tensor
        def _(pe):
            pe.wait_ge(w_in, 16 * w_count)
            if layer == 0:
                for b in range(NB):
                    for m, w in enumerate((wq, wk, wv)):
                        pe.matmul(bk[b][:, m, :], ones_row[:], rows[:, m * D:(m + 1) * D], start=True, stop=False)
                        for k in range(KD):
                            ins = pe.matmul(bk[b][:, m, :], normed_T[:, k, b * P:(b + 1) * P], w[:, k, :],
                                            start=False, stop=(k == KD - 1))
                        ins.then_inc(s["proj"], 1)
                for b in range(NB):
                    pe.wait_ge(s["rope"], 6 * (b + 1))
                    for m in range(2):
                        for k in range(KA):
                            ins = pe.transpose(bk[b][:, m, k * P:(k + 1) * P], turned[:, b, m, k * P:(k + 1) * P],
                                               ident[:])
                        ins.then_inc(s["qkT"], 1)
            else:
                for m, w in enumerate((wq, wk)):
                    for n in range(KA):
                        for k in range(KD):
                            ins = pe.matmul(bk[m][:, n // 2, (n % 2) * TOK:(n % 2 + 1) * TOK],
                                            w[:, k, n * P:(n + 1) * P], normed_T[:, k, :],
                                            start=(k == 0), stop=(k == KD - 1))
                        if n % 2:
                            ins.then_inc(s["qkT"], 1)
                for b in range(NB):
                    for m in range(NW):
                        pe.wait_ge(s["qkT_out"], 4 * b + m + 1)
                        for k in range(KD):
                            ins = pe.matmul(bk[b][:, m, :], normed_T[:, k, b * P:(b + 1) * P],
                                            wv[:, k, m * D:(m + 1) * D], start=(k == 0), stop=(k == KD - 1))
                        ins.then_inc(s["proj"], 1)
            for b in range(NB):
                if layer == 0:
                    pe.wait_ge(s["qkT_out"], 2 * (b + 1))
                    pe.wait_ge(s["v_out"], b + 1)
                else:
                    pe.wait_ge(s["qkT_out"], 8)
                    pe.wait_ge(s["v_out"], NW * (b + 1))
                for h in sorted(range(H), key=lambda h: place(h)):
                    bank, col = place(h)
                    r = slice((h % per) * dh, (h % per + 1) * dh)
                    ins = pe.matmul(bk[b][:, bank, col:col + P], qT[r, h // per, b * P:(b + 1) * P],
                                    kT[r, h // per, b * P:(b + 1) * P], start=True, stop=True)
                    if col == 3 * P:
                        ins.then_inc(s["score"], 1)
            for b in range(NB):
                pe.wait_ge(s["exped"], b + 1)
                for n in range(H):
                    ins = pe.transpose(bk[b][:, n // 4, (n % 4) * P:(n % 4 + 1) * P], sc[:, b, n * P:(n + 1) * P],
                                       ident[:])
                    if n % 4 == 3:
                        ins.then_inc(s["pT"], 1)
            for b in range(NB):
                pe.wait_ge(s["pT_out"], 4 * (b + 1))
                for h in range(H):
                    bank, col = place(h)
                    at = bank * 4 * P + col
                    ins = pe.matmul(bk[b][:, h * dh // D, h * dh % D:h * dh % D + dh], pT[:, b, at:at + P],
                                    v[:, b, h * dh:(h + 1) * dh], start=True, stop=True)
                ins.then_inc(s["pv"], 1)
            for b in range(NB):
                pe.wait_ge(s["normed"], b + 1)
                for k in range(KA):
                    ins = pe.transpose(bk[b][:, 2 + k // 4, (k % 4) * P:(k % 4 + 1) * P],
                                       attn[:, b, k * P:(k + 1) * P], ident[:])
                ins.then_inc(s["aT"], 1)
            pe.wait_ge(*env[f"{tag}_wp_in"])
            for b in range(NB):
                pe.wait_ge(s["aT_out"], b + 1)
                if layer == 0:
                    pe.matmul(bk[b][:, 0, :], ones_row[:], rows[:, 3 * D:4 * D], start=True, stop=False)
                for k in range(KA):
                    ins = pe.matmul(bk[b][:, 0, :], attn_T[:, k, b * P:(b + 1) * P], wp[:, k, :],
                                    start=(k == 0 and layer == 1), stop=(k == KA - 1))
                ins.then_inc(s["y"], 1)

        @block.scalar
        def _(act):
            if layer == 0:
                for b in range(NB):
                    act.wait_ge(s["proj"], 3 * b + 3)
                    act.activation(v[:, b, :], bk[b][:, 2, :], ACT.Copy).then_inc(s["v_out"], 1)
                for b in range(NB):
                    for m, dst in enumerate((qT, kT)):
                        act.wait_ge(s["qkT"], 2 * b + m + 1)
                        act.activation(dst[:, :, b * P:(b + 1) * P],
                                       bk[b][:, m, :].rearrange("p (k t) -> p k t", k=KA),
                                       ACT.Copy).then_inc(s["qkT_out"], 1)
            else:
                for m, dst in enumerate((qT, kT)):
                    for n in range(4):
                        act.wait_ge(s["qkT"], 4 * m + n + 1)
                        act.activation(dst[:, 2 * n:2 * n + 2, :],
                                       bk[m][:, n, :].rearrange("p (k t) -> p k t", k=2),
                                       ACT.Copy).then_inc(s["qkT_out"], 1)
                for b in range(NB):
                    for m in range(NW):
                        act.wait_ge(s["proj"], NW * b + m + 1)
                        act.activation(v[:, b, m * D:(m + 1) * D], bk[b][:, m, :], ACT.Copy).then_inc(s["v_out"], 1)
            for b in range(NB):
                act.wait_ge(s["shifted"], b + 1)
                act.activation(sc[:, b, :], sc[:, b, :], ACT.Exp, scale=scale).then_inc(s["exped"], 1)
            for b in range(NB):
                for n in range(4):
                    act.wait_ge(s["pT"], 4 * b + n + 1)
                    act.activation(pT[:, b, n * D:(n + 1) * D], bk[b][:, n, :], ACT.Copy).then_inc(s["pT_out"], 1)
            for b in range(NB):
                act.wait_ge(s["aT"], b + 1)
                act.activation(attn_T[:, :, b * P:(b + 1) * P],
                               bk[b][:, 2:4, :].rearrange("p u (k t) -> p (u k) t", t=P)[:, 0:KA, :],
                               ACT.Copy).then_inc(s["aT_out"], 1)

        @block.vector
        def _(dve):
            if layer == 0:
                dve.wait_ge(w_in, 16 * w_count)
                cc, ss = (t[:].rearrange("p (m n) -> p m n", m=2) for t in (rope_c, rope_s))
                for b in range(NB):
                    dve.wait_ge(s["proj"], 3 * b + 2)
                    pairs = bk[b][:, 0:2, :].rearrange("p m (n two) -> p m n two", two=2)
                    even, odd = pairs[:, :, :, 0], pairs[:, :, :, 1]
                    for i, (a, t) in enumerate(((even, cc), (odd, ss), (even, ss), (odd, cc))):
                        dve.tensor_tensor(part[:, b, i, :, :], a, t, ALU.mult).then_inc(s["rope"], 1)
                    dve.wait_ge(s["rope"], 6 * b + 4)
                    to = turned[:, b, :, :].rearrange("p m (n two) -> p m n two", two=2)
                    dve.tensor_tensor(to[:, :, :, 0], part[:, b, 0, :, :], part[:, b, 1, :, :],
                                      ALU.subtract).then_inc(s["rope"], 1)
                    dve.tensor_tensor(to[:, :, :, 1], part[:, b, 2, :, :], part[:, b, 3, :, :],
                                      ALU.add).then_inc(s["rope"], 1)
            else:
                dve.wait_ge(w_in, 16 * w_count)
            for b in range(NB):
                heads = sc[:, b, :].rearrange("p (h t) -> p h t", h=H)
                for n in range(4):
                    dve.wait_ge(s["score"], 4 * b + n + 1)
                    dve.tensor_tensor(sc[:, b, n * D:(n + 1) * D], bk[b][:, n, :], mask[:],
                                      ALU.add).then_inc(s["masked"], 1)
                dve.wait_ge(s["masked"], 4 * (b + 1))
                dve.tensor_reduce(stat[:, 0, b, :], heads, AX.X, ALU.max).then_inc(s["maxed"], 1)
                dve.wait_ge(s["maxed"], b + 1)
                dve.tensor_tensor(heads, heads, stat[:, 0, b, :].unsqueeze(2).broadcast_to([P, H, P]),
                                  ALU.subtract).then_inc(s["shifted"], 1)
            for b in range(NB):
                dve.wait_ge(s["exped"], b + 1)
                dve.tensor_reduce(stat[:, 1, b, :], sc[:, b, :].rearrange("p (h t) -> p h t", h=H), AX.X,
                                  ALU.add).then_inc(s["den"], 1)
                dve.wait_ge(s["den"], 2 * b + 1)
                dve.reciprocal(stat[:, 2, b, :], stat[:, 1, b, :]).then_inc(s["den"], 1)
            for b in range(NB):
                dve.wait_ge(s["pv"], b + 1)
                dve.wait_ge(s["den"], 2 * b + 2)
                inv = stat[:, 2, b, :].rearrange("p (r g) -> p g r", r=per).unsqueeze(3).broadcast_to([P, KA, per, dh])
                o = bk[b][:, 0:NW, :].rearrange("p u n -> p (u n)").rearrange("p (g r d) -> p g r d", g=KA, r=per)
                dve.tensor_tensor(attn[:, b, :].rearrange("p (g r d) -> p g r d", g=KA, r=per), o, inv,
                                  ALU.mult).then_inc(s["normed"], 1)
            for b in range(NB):
                dve.wait_ge(s["y"], b + 1)
                dve.tensor_tensor(resid[:, b, :], bk[b][:, 0, :], resid[:, b, :], ALU.add).then_inc(s["done"], 1)


def sign_layer(nc, I, env):
    sem, sb_in, ps_in = env["sem"], env["sb_in"], env["ps_in"]
    resid, normed_T = env["resid"], env["normed_T"]
    w, w_in, w_need = env["sgn_w"], env["sgn_w_in"], env["sgn_w_need"]
    signed, y_ready, done = sem("sg_signed"), sem("sg_y"), sem("sg_done")
    with nc.Block() as block:
        @block.scalar
        def _(act):
            act.wait_ge(w_in, w_need)
            act.activation(w[:], w[:], ACT.Sign).then_inc(signed, 1)
    env["layer_norm_T"]("sgln")
    with ExitStack() as st:
        y_ps = ps_in(st, "sg_y_ps", [P, NB, D])
        block = st.enter_context(nc.Block())

        @block.tensor
        def _(pe):
            pe.wait_ge(signed, 1)
            for b in range(NB):
                for k in range(KD):
                    ins = pe.matmul(y_ps[:, b, :], normed_T[:, k, b * P:(b + 1) * P], w[:, k, :],
                                    start=(k == 0), stop=(k == KD - 1))
                ins.then_inc(y_ready, 1)

        @block.vector
        def _(dve):
            for b in range(NB):
                dve.wait_ge(y_ready, b + 1)
                dve.tensor_tensor(resid[:, b, :], y_ps[:, b, :], resid[:, b, :], ALU.add).then_inc(done, 1)


def cross_attention_masked(nc, I, env):
    sem, sb_in, ps_in = env["sem"], env["sb_in"], env["ps_in"]
    resid, ident, ones_row, normed_T = env["resid"], env["ident"], env["ones_row"], env["normed_T"]
    wo, wo_row, w_in = env["wo1"], env["wo1_row"], sem("x1_wo_in")
    s = {n: sem("x1_" + n) for n in
         ("k_in0", "k_in1", "v_in0", "v_in1", "m_in0", "m_in1", "k_hi", "k_lo", "zeroed", "q_hi", "q_lo", "score", "masked",
          "top", "topped", "exped", "den", "pT", "pT_out", "pv", "sel", "part", "out", "normed", "aT", "aT_out", "y", "q_grp", "mask_cur",
          "act_y", "done")}
    SC0, PV0, PT0, CP0 = 17, 17, 8, 4
    env["layer_norm_T"]("x1ln")
    with ExitStack() as st:
        attn = sb_in(st, "x1_attn", [P, NB, D])
        attn_T = sb_in(st, "x1_attn_T", [P, KD, TOK])
        attn_flat = attn[:].rearrange("p b n -> p (b n)")
        with ExitStack() as st2:
            mask = sb_in(st2, "x1_mask", [P, NB * S])
            mask_cur = sb_in(st2, "x1_mask_cur", [P, S])
            q_grp = sb_in(st2, "x1_q_grp", [P, NB * 4 * P])
            k_raw = sb_in(st2, "x1_k_raw", [P, 2, S])
            keys = sb_in(st2, "x1_keys", [P, 2, 2, S], F32R)
            val = sb_in(st2, "x1_val", [P, 2, NCH, P])
            q_hi = sb_in(st2, "x1_q_hi", [P, 2, 4, P], F32R)
            q_lo = sb_in(st2, "x1_q_lo", [P, 2, 4, P], F32R)
            sc = sb_in(st2, "x1_sc", [P, 2, S])
            pT = sb_in(st2, "x1_pT", [P, 4, 512])
            tops = sb_in(st2, "x1_tops", [P, 2, 4])
            part = sb_in(st2, "x1_part", [P, 2, P])
            sel = sb_in(st2, "x1_sel", [P, DHS])
            half_sel = sb_in(st2, "x1_half_sel", [P, 2, DHS])
            gate = sb_in(st2, "x1_gate", [1, 3, 4])
            negtop = sb_in(st2, "x1_negtop", [P, 2])
            den = sb_in(st2, "x1_den", [P, 4, 2])
            dsum = sb_in(st2, "x1_dsum", [P, 2])
            rden = sb_in(st2, "x1_rden", [P, 2])
            s_ps = ps_in(st2, "x1_s_ps", [P, 4, 512])
            t_ps = ps_in(st2, "x1_t_ps", [P, 2, 512])
            o_ps = ps_in(st2, "x1_o_ps", [P, 2, 512])
            block = st2.enter_context(nc.Block())

            def at(i, t):
                return (i + 1, t - 8) if t >= 8 else (i, t)

            @block.sync
            def _(sp):
                def load(i, first=False):
                    for r in range(2):
                        G = i * 2 + r
                        for m in range(2):
                            sp.wait_ge(s["k_lo"], G * 2 + (m + 1))
                            for copy in range(2):
                                sp.dma_start(k_raw[64 * copy:64 * copy + 64, m, :],
                                             I["ctx_T"][bass.ds(G * P + 64 * m, 64), :]).then_inc(s[f"k_in{m}"], 16)
                            if first and r == 0 and m == 0:
                                sp.dma_start(mask[:, 0:S], I["mask"][0]).then_inc(s["m_in0"], 16)
                        sp.wait_ge(s["pv"], G * 16 + 1)
                        sp.dma_start(val[:, r, :, :], I["ctx_heads"][bass.ds(G * P, P), :]
                                     .rearrange("p (c n) -> p c n", c=NCH)).then_inc(s[f"v_in{r}"], 16)
                load(0, first=True)
                for b in range(1, NB):
                    sp.dma_start(mask[:, b * S:(b + 1) * S], I["mask"][b]).then_inc(s[f"m_in{b}"], 16)
                sp.dma_start(wo[:], I["wo1"].rearrange("(k p) n -> p k n", p=P)).then_inc(w_in, 16)
                sp.dma_start(wo_row[:], I["wo1_row"]).then_inc(w_in, 16)
                with sp.Fori(1, 4) as i:
                    load(i)

            @block.gpsimd
            def _(pool):
                pool.memset(q_hi[:].bitcast(F32), 0.0).then_inc(s["zeroed"], 1)
                pool.memset(q_lo[:].bitcast(F32), 0.0).then_inc(s["zeroed"], 1)
                pool.memset(gate[:], 0.0).then_inc(s["zeroed"], 1)
                pool.sem_inc(s["k_lo"], 2)
                with pool.Fori(0, 4) as i:
                    for r in range(2):
                        G = i * 2 + r
                        for m in range(2):
                            pool.wait_ge(s["k_hi"], G * 2 + (m + 1))
                            pool.tensor_tensor(keys[64:, r, m, :], k_raw[64:, m, :], keys[64:, r, m, :],
                                               ALU.subtract).then_inc(s["k_lo"], 1)

            @block.vector
            def _(dve):
                dve.wait_ge(s["zeroed"], 3)
                for b in range(NB):
                    dve.tensor_copy(q_grp[:, b * 4 * P:(b + 1) * 4 * P].rearrange("p (k t) -> p k t", k=KD),
                                    normed_T[:, :, b * P:(b + 1) * P]).then_inc(s["q_grp"], 1)
                dve.wait_ge(s["q_grp"], 2)
                for n in range(2):
                    dve.tensor_tensor(half_sel[:, n, :], ident[:, 2 * n * DHS:(2 * n + 1) * DHS],
                                      ident[:, (2 * n + 1) * DHS:(2 * n + 2) * DHS], ALU.add).then_inc(s["sel"], 1)
                dve.wait_ge(s["sel"], 2)
                dve.tensor_tensor(sel[:], half_sel[:, 0, :], half_sel[:, 1, :], ALU.add).then_inc(s["sel"], 1)

                def prepare_keys(i, r, m):
                    G = i * 2 + r
                    dve.wait_ge(s[f"k_in{m}"], G * 32 + 32)
                    dve.wait_ge(s["score"], G * 16 + (8 * m + 1))
                    dve.tensor_copy(keys[:, r, m, :], k_raw[:, m, :]).then_inc(s["k_hi"], 1)

                copies = [(j, slice(32 * (j % 2) + 64 * half, 32 * (j % 2) + 64 * half + 32))
                          for j in range(4) for half in range(2)]

                def queries_high(i, r):
                    G = i * 2 + r
                    for j, rows in copies:
                        dve.tensor_copy(q_hi[rows, r, j, :],
                                        q_grp[32 * j:32 * j + 32, bass.ds(G * P, P)]).then_inc(s["q_hi"], 1)

                def queries_low(i, r):
                    G = i * 2 + r
                    dve.wait_ge(s["q_hi"], G * 8 + 8)
                    for j, rows in copies:
                        dve.tensor_tensor(q_lo[rows, r, j, :], q_grp[32 * j:32 * j + 32, bass.ds(G * P, P)],
                                          q_hi[32 * j:32 * j + 32, r, j, :], ALU.subtract).then_inc(s["q_lo"], 1)

                def new_mask(i):
                    dve.tensor_copy(mask_cur[:], mask[:, bass.ds((i // 2) * S, S)]).then_inc(s["mask_cur"], 1)
                    dve.wait_ge(s["mask_cur"], i + 1)

                def masked(i, t, c):
                    hd = i * 8 + t
                    dve.wait_ge(s["pT"], hd * 4 + (PT0 + c - 7))
                    dve.wait_ge(s["score"], hd * 4 + (SC0 + c + 1))
                    dve.tensor_copy(gate[0:1, t % 2, c:c + 1], gate[0:1, 2, 0:1])
                    dve.tensor_tensor_reduce(sc[:, t % 2, c * 512:(c + 1) * 512], s_ps[:, c, :],
                                             mask_cur[:, c * 512:(c + 1) * 512], 1.0, -3.0e38, ALU.add,
                                             ALU.max, tops[:, t % 2, c:c + 1]).then_inc(s["masked"], 1)

                def top(i, t):
                    hd = i * 8 + t
                    dve.wait_ge(s["masked"], hd * 4 + 4)
                    dve.tensor_reduce(negtop[:, t % 2:t % 2 + 1], tops[:, t % 2, :], AX.X, ALU.max,
                                      negate=True).then_inc(s["top"], 1)

                def collect(i, t):
                    hd = i * 8 + t
                    dve.wait_ge(s["pv"], hd * 4 + (PV0 + 4))
                    dve.tensor_copy(part[:, t % 2, :], o_ps[:, t % 2, 0:P]).then_inc(s["part"], 1)

                def normalise(i, t):
                    hd = i * 8 + t
                    o = t % 2
                    dve.wait_ge(s["exped"], hd * 2 + 2)
                    dve.tensor_tensor(dsum[:, o:o + 1], den[:, t % 4, 0:1], den[:, t % 4, 1:2], ALU.add).then_inc(s["den"], 1)
                    dve.wait_ge(s["den"], hd * 2 + 1)
                    dve.reciprocal(rden[:, o:o + 1], dsum[:, o:o + 1]).then_inc(s["den"], 1)
                    dve.wait_ge(s["den"], hd * 2 + 2)
                    dve.wait_ge(s["out"], hd + 1)
                    dve.tensor_scalar(attn_flat[:, bass.ds(hd * DHS, DHS)], o_ps[:, o, P:P + DHS],
                                      rden[:, o:o + 1], None, ALU.mult).then_inc(s["normed"], 1)

                def heads(i, last=False):
                    for t in range(8):
                        two = t + 2 < 8 or not last
                        if two:
                            if t == 6:
                                new_mask(i + 1)
                            masked(*at(i, t + 2), 0)
                        if t == 0:
                            prepare_keys(i, 1, 1)
                        elif t == 1:
                            queries_low(i, 1)
                        elif t in (2, 4) and not last:
                            prepare_keys(i + 1, 0, t // 4)
                        elif t == 3 and not last:
                            queries_high(i + 1, 0)
                        elif t == 5 and not last:
                            queries_low(i + 1, 0)
                        elif t == 6 and not last:
                            queries_high(i + 1, 1)
                        elif t == 7 and not last:
                            prepare_keys(i + 1, 1, 0)
                        if two:
                            masked(*at(i, t + 2), 1)
                        collect(i, t)
                        if two:
                            masked(*at(i, t + 2), 2)
                            masked(*at(i, t + 2), 3)
                            top(*at(i, t + 2))
                        normalise(i, t)
                queries_high(0, 0)
                queries_low(0, 0)
                prepare_keys(0, 0, 0)
                queries_high(0, 1)
                prepare_keys(0, 0, 1)
                dve.wait_ge(s["m_in0"], 16)
                new_mask(0)
                for c in range(4):
                    masked(0, 0, c)
                top(0, 0)
                masked(0, 1, 0)
                prepare_keys(0, 1, 0)
                for c in range(1, 4):
                    masked(0, 1, c)
                top(0, 1)
                dve.wait_ge(s["m_in1"], 16)
                with dve.Fori(0, 3) as i:
                    heads(i)
                heads(3, last=True)

            @block.scalar
            def _(act):
                def exp(i, t, half):
                    hd = i * 8 + t
                    if half == 0:
                        act.wait_ge(s["top"], hd + 1)
                        act.wait_ge(s["normed"], hd + 1)
                    part = sc[:, t % 2, half * (S // 2):(half + 1) * (S // 2)]
                    act.activation(part, part, ACT.Exp, bias=negtop[:, t % 2:t % 2 + 1],
                                   accum_out=den[:, t % 4, half:half + 1]).then_inc(s["exped"], 1)

                def evacuate(i, t, c):
                    hd = i * 8 + t
                    act.wait_ge(s["pT"], hd * 4 + (PT0 + c + 1))
                    act.wait_ge(s["pv"], hd * 4 + (PV0 + c - 3))
                    act.activation(pT[:, c, :], t_ps[:, c % 2, :], ACT.Copy).then_inc(s["pT_out"], 1)

                def heads(i, last=False):
                    for t in range(8):
                        one = t + 1 < 8 or not last
                        for c in range(3):
                            evacuate(i, t, c)
                        if one:
                            exp(*at(i, t + 1), 0)
                        evacuate(i, t, 3)
                        if one:
                            exp(*at(i, t + 1), 1)
                exp(0, 0, 0)
                exp(0, 0, 1)
                with act.Fori(0, 3) as i:
                    heads(i)
                heads(3, last=True)

            @block.tensor
            def _(pe):
                pe.sem_inc(s["score"], SC0)
                pe.sem_inc(s["pv"], PV0)
                pe.sem_inc(s["pT"], PT0)
                pe.sem_inc(s["pT_out"], CP0)
                pe.sem_inc(s["normed"], 4)

                def scores(i, t, c, first=False):
                    hd = i * 8 + t
                    r, j = t // 4, t % 4
                    if j % 2 == 0 and c == 0:
                        pe.wait_ge(s["k_lo"], i * 4 + (r * 2 + j // 2 + 3))
                        pe.wait_ge(s["q_lo"], i * 16 + (r * 8 + 8))
                    if not first:
                        pe.wait_ge(s["masked"], hd * 4 + (c - 3))
                    pair = keys[:, r, j // 2, c * 512:(c + 1) * 512]
                    pe.matmul(s_ps[:, c, :], q_lo[:, r, j, :], pair, start=True, stop=False)
                    pe.matmul(s_ps[:, c, :], q_hi[:, r, j, :], pair, start=False, stop=True).then_inc(s["score"], 1)

                def turn(i, t, c):
                    hd = i * 8 + t
                    if c % 2 == 0:
                        pe.wait_ge(s["exped"], hd * 2 + (c // 2 + 1))
                    pe.wait_ge(s["pT_out"], hd * 4 + (CP0 + c - 1))
                    for k in range(4):
                        ins = pe.transpose(t_ps[:, c % 2, k * P:(k + 1) * P],
                                           sc[:, t % 2, (4 * c + k) * P:(4 * c + k + 1) * P], ident[:])
                    ins.then_inc(s["pT"], 1)

                def weigh(i, t, c):
                    hd = i * 8 + t
                    r, j = t // 4, t % 4
                    if c == 0:
                        pe.wait_ge(s["normed"], hd + 3)
                        if j == 0:
                            pe.wait_ge(s[f"v_in{r}"], i * 16 + 16)
                    pe.wait_ge(s["pT_out"], hd * 4 + (CP0 + c + 1))
                    for k in range(4):
                        ins = pe.matmul(o_ps[32 * k:32 * k + 32, t % 2, 0:P],
                                        val[:, r, 4 * c + k, j * DHS:(j + 1) * DHS], pT[:, c, k * P:(k + 1) * P],
                                        start=(c == 0), stop=(c == 3), tile_position=(0, 32 * k))
                    ins.then_inc(s["pv"], 1)

                def gather(i, t):
                    hd = i * 8 + t
                    pe.wait_ge(s["part"], hd + 1)
                    pe.matmul(o_ps[:, t % 2, P:P + DHS], part[:, t % 2, :], sel[:], start=True,
                              stop=True).then_inc(s["out"], 1)

                def heads(i, last=False):
                    for t in range(8):
                        one, two = t + 1 < 8 or not last, t + 2 < 8 or not last
                        for c in range(4):
                            if two:
                                scores(*at(i, t + 2), c)
                            if c == 0:
                                turn(i, t, 3)
                            elif one:
                                turn(*at(i, t + 1), c - 1)
                            if c < 2:
                                weigh(i, t, c + 2)
                            elif one:
                                weigh(*at(i, t + 1), c - 2)
                        gather(i, t)
                pe.wait_ge(s["sel"], 3)
                for c in range(4):
                    scores(0, 0, c, first=True)
                scores(0, 1, 0)
                scores(0, 1, 1)
                turn(0, 0, 0)
                for c in range(2):
                    scores(0, 1, c + 2)
                    turn(0, 0, c + 1)
                    weigh(0, 0, c)
                with pe.Fori(0, 3) as i:
                    heads(i)
                heads(3, last=True)
        with ExitStack() as st2:
            a_ps = ps_in(st2, "x1_a_ps", [P, 2, 2, TOK])
            y_ps = ps_in(st2, "x1_y_ps", [P, NB, D])
            y = sb_in(st2, "x1_y", [P, NB, D])
            block = st2.enter_context(nc.Block())

            @block.tensor
            def _(pe):
                for n in range(2):
                    for c in range(2):
                        for b in range(NB):
                            k = 2 * n + c
                            ins = pe.transpose(a_ps[:, n, c, b * P:(b + 1) * P], attn[:, b, k * P:(k + 1) * P],
                                               ident[:])
                    ins.then_inc(s["aT"], 1)
                pe.wait_ge(w_in, 32)
                for b in range(NB):
                    pe.matmul(y_ps[:, b, :], ones_row[:], wo_row[:], start=True, stop=False)
                    for k in range(KD):
                        if b == 0 and k % 2 == 0:
                            pe.wait_ge(s["aT_out"], k // 2 + 1)
                        ins = pe.matmul(y_ps[:, b, :], attn_T[:, k, b * P:(b + 1) * P], wo[:, k, :],
                                        start=False, stop=(k == KD - 1))
                    ins.then_inc(s["y"], 1)

            @block.scalar
            def _(act):
                for n in range(2):
                    act.wait_ge(s["aT"], n + 1)
                    act.activation(attn_T[:, 2 * n:2 * n + 2, :], a_ps[:, n, :, :], ACT.Copy).then_inc(s["aT_out"], 1)
                for b in range(NB):
                    act.wait_ge(s["y"], b + 1)
                    act.activation(y[:, b, :], y_ps[:, b, :], ACT.Relu).then_inc(s["act_y"], 1)

            @block.vector
            def _(dve):
                for b in range(NB):
                    dve.wait_ge(s["act_y"], b + 1)
                    dve.tensor_tensor(resid[:, b, :], y[:, b, :], resid[:, b, :], ALU.add).then_inc(s["done"], 1)


def experts(nc, I, env):
    sem, sb_in, ps_in = env["sem"], env["sb_in"], env["ps_in"]
    resid, normed_T, ones_row, ident = env["resid"], env["normed_T"], env["ones_row"], env["ident"]
    w1_raw, w2_raw, s1, s2 = env["w1_raw"], env["w2_raw"], env["w1_in"], env["w2_in"]
    E, NP = E_MOE, 4
    s = {n: sem("mo_" + n) for n in
         ("small_in", "logit", "step", "exp", "rT", "rT_out", "bias", "acc", "w1_hi", "w1_lo", "w2_hi", "w2_lo",
          "h_mm", "gelu", "h_hi", "h_lo", "y_mm", "x_hi", "x_lo", "b1", "r_cur", "added")}
    env["layer_norm_T"]("moln")
    with ExitStack() as st:
        wr = sb_in(st, "mo_wr", [P, KD, E])
        br = sb_in(st, "mo_br", [1, E])
        b2 = sb_in(st, "mo_b2", [E, D])
        b1 = sb_in(st, "mo_b1", [P, E * 16])
        b1_cur = sb_in(st, "mo_b1_cur", [P, 2, 4])
        before = sb_in(st, "mo_before", [P, E * E])
        logit = sb_in(st, "mo_logit", [P, NB, E])
        cmp_a = sb_in(st, "mo_cmp_a", [P, NB, E, E])
        cmp_b = sb_in(st, "mo_cmp_b", [P, NB, E, E])
        rank = sb_in(st, "mo_rank", [P, NB, E])
        stat = sb_in(st, "mo_stat", [P, 3, NB])
        route = sb_in(st, "mo_route", [P, NB, E])
        r_cur = sb_in(st, "mo_r_cur", [P, NB])
        route_T = sb_in(st, "mo_route_T", [E, NB, P])
        x_hi = sb_in(st, "mo_x_hi", [P, KD, TOK], F32R)
        x_lo = sb_in(st, "mo_x_lo", [P, KD, TOK], F32R)
        w1_hi = sb_in(st, "mo_w1_hi", [P, 2, KD, 512], F32R)
        w1_lo = sb_in(st, "mo_w1_lo", [P, 2, KD, 512], F32R)
        w2_hi = sb_in(st, "mo_w2_hi", [P, 2, NP, D], F32R)
        w2_lo = sb_in(st, "mo_w2_lo", [P, 2, NP, D], F32R)
        hid = sb_in(st, "mo_hid", [P, 2, NP, TOK])
        h_hi = sb_in(st, "mo_h_hi", [P, 2, NP, TOK], F32R)
        h_lo = sb_in(st, "mo_h_lo", [P, 2, NP, TOK], F32R)
        h_ps = ps_in(st, "mo_h_ps", [P, 4, 512])
        y_ps = ps_in(st, "mo_y_ps", [P, 2, NB, D])
        with nc.Block() as block:
            @block.gpsimd
            def _(pool):
                for dst, name in ((wr[:], "wr"), (br[:], "br"), (b2[:], "b2"), (b1[:], "b1"), (before[:], "before")):
                    pool.dma_start(dst, I[name]).then_inc(s["small_in"], 16)

            @block.tensor
            def _(pe):
                pe.wait_ge(s["small_in"], 16 * 5)
                for b in range(NB):
                    lg = y_ps[:, 0, b, 0:E]
                    pe.matmul(lg, ones_row[:], br[:], start=True, stop=False)
                    for k in range(KD):
                        ins = pe.matmul(lg, normed_T[:, k, b * P:(b + 1) * P], wr[:, k, :], start=False,
                                        stop=(k == KD - 1))
                ins.then_inc(s["logit"], 1)
                pe.wait_ge(s["step"], 17)
                for b in range(NB):
                    ins = pe.transpose(h_ps[0:E, 0, b * P:(b + 1) * P], route[:, b, :], ident[:])
                ins.then_inc(s["rT"], 1)
                pe.wait_ge(s["rT_out"], 1)
                for b in range(NB):
                    ins = pe.matmul(y_ps[:, 1, b, :], route_T[:, b, :], b2[:], start=True, stop=True)
                ins.then_inc(s["bias"], 1)

            @block.scalar
            def _(act):
                act.activation(x_hi[:], normed_T[:], ACT.Copy).then_inc(s["x_hi"], 1)
                act.wait_ge(s["step"], 10)
                act.activation(route[:], logit[:], ACT.Exp).then_inc(s["exp"], 1)

            @block.vector
            def _(dve):
                dve.wait_ge(s["x_hi"], 1)
                dve.tensor_tensor(x_lo[:], normed_T[:], x_hi[:], ALU.subtract).then_inc(s["x_lo"], 1)
                step = Chain(dve, s["step"])
                dve.wait_ge(s["logit"], 1)
                step(dve.tensor_copy(logit[:], y_ps[:, 0, :, 0:E]))
                for b in range(NB):
                    other = logit[:, b, :].unsqueeze(1).broadcast_to([P, E, E])
                    own = logit[:, b, :].unsqueeze(2).broadcast_to([P, E, E])
                    dve.tensor_tensor(cmp_a[:, b, :, :], other, own, ALU.is_gt).then_inc(s["step"], 1)
                    dve.tensor_tensor(cmp_b[:, b, :, :], other, own, ALU.is_equal).then_inc(s["step"], 1)
                step.n += 4
                dve.wait_ge(s["step"], step.n)
                low = before[:].rearrange("p (e f) -> p e f", e=E).unsqueeze(1).broadcast_to([P, NB, E, E])
                flat = lambda t: t[:].rearrange("p b e f -> p (b e) f")
                step(dve.tensor_tensor(cmp_b[:], cmp_b[:], low, ALU.mult))
                step(dve.tensor_tensor(flat(cmp_a), flat(cmp_a), flat(cmp_b), ALU.add))
                step(dve.tensor_reduce(rank[:].rearrange("p b e -> p (b e)"), flat(cmp_a), AX.X, ALU.add))
                step(dve.tensor_reduce(stat[:, 0, :], logit[:], AX.X, ALU.max))
                step(dve.tensor_tensor(logit[:], logit[:], stat[:, 0, :].unsqueeze(2).broadcast_to([P, NB, E]),
                                       ALU.subtract))
                dve.wait_ge(s["exp"], 1)
                step(dve.tensor_scalar(rank[:], rank[:], 2.0, None, ALU.is_lt))
                step(dve.tensor_tensor(route[:], route[:], rank[:], ALU.mult))
                step(dve.tensor_reduce(stat[:, 1, :], route[:], AX.X, ALU.add))
                step(dve.reciprocal(stat[:, 2, :], stat[:, 1, :]))
                step(dve.tensor_tensor(route[:], route[:], stat[:, 2, :].unsqueeze(2).broadcast_to([P, NB, E]),
                                       ALU.mult))
                step(dve.memset(r_cur[:], 0.0))
                step(dve.memset(b1_cur[:], 0.0))
                assert step.n == 17
                dve.wait_ge(s["rT"], 1)
                dve.tensor_copy(route_T[:], h_ps[0:E, 0, 0:TOK].rearrange("e (b t) -> e b t", b=NB))\
                    .then_inc(s["rT_out"], 1)
                dve.wait_ge(s["bias"], 1)
                for b in range(NB):
                    dve.tensor_tensor(resid[:, b, :], y_ps[:, 1, b, :], resid[:, b, :], ALU.add).then_inc(s["acc"], 1)

        block = st.enter_context(nc.Block())

        @block.sync
        def _(sp):
            def load(e, j):
                U = e * NU + j
                sp.wait_ge(s["w1_lo"], U - 1)
                sp.dma_start(w1_raw[:, j % 2, :, :], I["w1"][bass.ds(U * P, P), :]
                             .rearrange("p (k n) -> p k n", k=KD)).then_inc(s1[j % 2], 16)
                sp.wait_ge(s["w2_lo"], U - 1)
                sp.dma_start(w2_raw[:, j % 2, :, :], I["w2"][bass.ds(U * P, P), :]
                             .rearrange("p (k n) -> p k n", k=NP)).then_inc(s2[j % 2], 16)
            for j in (2, 3):
                load(0, j)
            with sp.Fori(1, E) as e:
                for j in range(NU):
                    load(e, j)

        @block.scalar
        def _(act):
            def high1(e, j, first=False):
                U, r = e * NU + j, j % 2
                act.wait_ge(s1[r], e * 32 + 16 * (j // 2 + 1))
                if not first:
                    act.wait_ge(s["h_mm"], U * NP - NP)
                act.activation(w1_hi[:, r, :, :], w1_raw[:, r, :, :], ACT.Copy).then_inc(s["w1_hi"], 1)

            def high2(e, j, first=False):
                U, r = e * NU + j, j % 2
                act.wait_ge(s2[r], e * 32 + 16 * (j // 2 + 1))
                if not first:
                    act.wait_ge(s["y_mm"], U - 1)
                act.activation(w2_hi[:, r, :, :], w2_raw[:, r, :, :], ACT.Copy).then_inc(s["w2_hi"], 1)

            def gelu(e, j):
                U, r = e * NU + j, j % 2
                act.wait_ge(s["b1"], U + 1)
                act.wait_ge(s["h_lo"], U + 1)
                for n in range(NP):
                    act.wait_ge(s["h_mm"], U * NP + (n // 2 * 2 + 2))
                    act.activation(hid[:, r, n, :], h_ps[:, 2 * r + n // 2, (n % 2) * TOK:(n % 2 + 1) * TOK],
                                   ACT.Gelu_apprx_tanh, bias=b1_cur[:, r, n:n + 1]).then_inc(s["gelu"], 1)

            high1(0, 0, True)
            high1(0, 1, True)
            high2(0, 0, True)

            def expert(e, first=False, last=False):
                for j in range(NU):
                    gelu(e, j)
                    if not (last and j >= 2):
                        high1(e, j + 2)
                    if not (last and j == 3):
                        high2(e, j + 1, first and j == 0)
            expert(0, first=True)
            with act.Fori(1, E - 1) as e:
                expert(e)
            expert(E - 1, last=True)

        @block.vector
        def _(dve):
            dve.sem_inc(s["h_lo"], 2)
            dve.sem_inc(s["added"], 1)

            def low1(e, j):
                U, r = e * NU + j, j % 2
                dve.wait_ge(s["w1_hi"], U + 1)
                dve.tensor_tensor(w1_lo[:, r, :, :], w1_raw[:, r, :, :], w1_hi[:, r, :, :],
                                  ALU.subtract).then_inc(s["w1_lo"], 1)

            def low2(e, j):
                U, r = e * NU + j, j % 2
                dve.wait_ge(s["w2_hi"], U + 1)
                dve.tensor_tensor(w2_lo[:, r, :, :], w2_raw[:, r, :, :], w2_hi[:, r, :, :],
                                  ALU.subtract).then_inc(s["w2_lo"], 1)

            def bias(e, j, first):
                U = e * NU + j
                if not first:
                    dve.wait_ge(s["gelu"], U * NP - NP)
                dve.tensor_copy(b1_cur[:, j % 2, :], b1[:, bass.ds(U * NP, NP)]).then_inc(s["b1"], 1)

            def split(e, j, first):
                U, r = e * NU + j, j % 2
                if not first:
                    dve.wait_ge(s["y_mm"], U - 1)
                dve.wait_ge(s["gelu"], U * NP + NP)
                dve.tensor_copy(h_hi[:, r, :, :], hid[:, r, :, :]).then_inc(s["h_hi"], 1)
                dve.wait_ge(s["h_hi"], U + 1)
                dve.tensor_tensor(h_lo[:, r, :, :], hid[:, r, :, :], h_hi[:, r, :, :],
                                  ALU.subtract).then_inc(s["h_lo"], 1)

            def combine(e, par):
                dve.tensor_copy(r_cur[:], route[:, :, bass.ds(e, 1)].rearrange("p b o -> p (b o)"))\
                    .then_inc(s["r_cur"], 1)
                dve.wait_ge(s["r_cur"], e + 1)
                dve.wait_ge(s["y_mm"], e * NU + NU)
                for b in range(NB):
                    dve.scalar_tensor_tensor(resid[:, b, :], y_ps[:, par, b, :], r_cur[:, b:b + 1],
                                             resid[:, b, :], ALU.mult, ALU.add).then_inc(s["added"], 1)
                dve.wait_ge(s["added"], e * NB + (NB + 1))
            low1(0, 0)
            low1(0, 1)
            low2(0, 0)
            bias(0, 0, True)

            def unit(e, j, first=False, last=False):
                if not (last and j == 3):
                    bias(e, j + 1, first and j == 0)
                split(e, j, first and j < 2)
                if not (last and j >= 2):
                    low1(e, j + 2)
                if not (last and j == 3):
                    low2(e, j + 1)
            for j in range(NU):
                unit(0, j, first=True)
            with dve.Fori(0, E // 2 - 1) as i:
                for half in range(2):
                    e = i * 2 + half
                    for j in range(NU):
                        unit(e + 1, j)
                        if j == 0:
                            combine(e, half)
            for j in range(NU):
                unit(E - 1, j, last=True)
                if j == 0:
                    combine(E - 2, 0)
            combine(E - 1, 1)

        @block.tensor
        def _(pe):
            def hidden(e, j, first=False):
                U, r = e * NU + j, j % 2
                pe.wait_ge(s["w1_lo"], U + 1)
                if not first:
                    pe.wait_ge(s["gelu"], U * NP - NP)
                for n in range(NP):
                    for k in range(KD):
                        ins = split_matmul(pe, h_ps[:, 2 * r + n // 2, (n % 2) * TOK:(n % 2 + 1) * TOK],
                                           w1_hi[:, r, k, n * P:(n + 1) * P], w1_lo[:, r, k, n * P:(n + 1) * P],
                                           x_hi[:, k, :], x_lo[:, k, :], k == 0, k == KD - 1)
                    ins.then_inc(s["h_mm"], 1)

            def output(e, j, par, first=False):
                U, r = e * NU + j, j % 2
                if j == 0 and not first:
                    pe.wait_ge(s["added"], e * NB - (NB - 1))
                pe.wait_ge(s["w2_lo"], U + 1)
                pe.wait_ge(s["h_lo"], U + 3)
                for b in range(NB):
                    for n in range(NP):
                        ins = split_matmul(pe, y_ps[:, par, b, :], h_hi[:, r, n, b * P:(b + 1) * P],
                                           h_lo[:, r, n, b * P:(b + 1) * P], w2_hi[:, r, n, :], w2_lo[:, r, n, :],
                                           j == 0 and n == 0, j == NU - 1 and n == NP - 1)
                ins.then_inc(s["y_mm"], 1)
            hidden(0, 0, first=True)

            def expert(e, par, first=False, last=False):
                for j in range(NU):
                    if not (last and j == NU - 1):
                        hidden(e, j + 1, first and j == 0)
                    output(e, j, par, first)
            expert(0, 0, first=True)
            with pe.Fori(0, E // 2 - 1) as i:
                for half in range(2):
                    expert(i * 2 + half + 1, 1 - half)
            expert(E - 1, 1, last=True)


STOP = 9


def kernel(**inputs):
    import numpy as np
    import concourse.bacc as bacc
    from concourse.bass_utils import run_bass_kernel_spmd

    x = {k: np.asarray(v) for k, v in inputs.items()}
    cols = lambda a: a.reshape(-1, 4, 128).transpose(0, 2, 1).reshape(-1, 128, 4)
    sign = np.repeat(np.array([0.125, 0.125, 0.125, -0.125], np.float32), 32)[:, None]
    vecs = np.concatenate([cols(x["L0_xattn_" + n])[0] for n in ("ln_lat_g", "ln_lat_b", "ln_ctx_g", "ln_ctx_b")]
                          + [sign], axis=1)
    wq = x["L0_xattn_Wq"].reshape(512, 16, 2, 32)[:, :, [0, 1, 1, 0], :].reshape(512, 2048)

    def quads(w):
        return w.reshape(4, 128, 4, 256).transpose(2, 1, 0, 3).reshape(4 * 128, 1024)

    wk, wv = quads(x["L0_xattn_Wkv"][:, :1024]), quads(x["L0_xattn_Wkv"][:, 1024:])
    theta = 1.0 / np.float32(10000.0) ** (np.float32(2.0) * np.arange(16, dtype=np.float32) / np.float32(32))
    angle = np.arange(128, dtype=np.float32)[:, None] * theta[None, :].astype(np.float32)
    rope = np.cos(angle).astype(np.float32), np.sin(angle).astype(np.float32)
    arrays = {
        "x": x["x"], "ident": np.eye(128, dtype=np.float32), "vecs": vecs, "wq_stack": wq,
        "cos_T4": np.tile(x["L0_xattn_cos"].T, (4, 1)), "sin_T4": np.tile(x["L0_xattn_sin"].T, (4, 1)),
        "ctx_rows": x["ctx_1024"].reshape(4096, 512),
        "wk_rows": wk, "wv_rows": np.concatenate([wv, wv[:128]]), "wo0": x["L0_xattn_Wo"],
        "bo0": x["L0_xattn_bo"][None],
        "causal4": np.tile(np.where(np.tril(np.ones((128, 128), bool)), 0, MASKED).astype(np.float32), (1, 4)),
        "sa0_wq": x["L0_attn_wq"].T, "sa0_wk": x["L0_attn_wk"].T, "sa0_wv": x["L0_attn_wv"].T,
        "sa0_wp": x["L0_attn_wp"].T,
        "sa0_rows": np.concatenate([x["L0_attn_b" + n] for n in "qkvp"])[None],
        "sa0_rc": np.tile(rope[0], (1, 32)), "sa0_rs": np.tile(rope[1], (1, 32)),
        "sgn_w": x["L0_ffn_weight"].T,
        "mask": x["mask_Bx1xSxS2_ff0"].reshape(2, 128, 2048),
        "ctx_T": x["ctx_1024"].transpose(0, 2, 1).reshape(1024, 2048),
        "ctx_heads": x["ctx_1024"].reshape(2, 16, 128, 4, 128).transpose(0, 3, 2, 1, 4).reshape(1024, 2048),
        "wo1": x["L1_xattn_wo_w"].T, "wo1_row": x["L1_xattn_wo_b"][None],
        "sa1_wq": x["L1_attn_query_mat"].reshape(512, 1024), "sa1_wk": x["L1_attn_key_mat"].reshape(512, 1024),
        "sa1_wv": x["L1_attn_value_mat"].reshape(512, 1024), "sa1_wp": x["L1_attn_linear_m1"],
        "w1": x["L1_ffn_W1"].reshape(8, 4, 128, 4, 512).transpose(0, 3, 2, 1, 4).reshape(4096, 2048),
        "w2": x["L1_ffn_W2"].reshape(8, 4, 4, 128, 512).transpose(0, 1, 3, 2, 4).reshape(4096, 2048),
        "b1": x["L1_ffn_b1"].reshape(128, 128).T, "b2": x["L1_ffn_b2"],
        "wr": x["L1_ffn_Wr"].reshape(4, 128, 8).transpose(1, 0, 2), "br": x["L1_ffn_br"][None],
        "before": np.tile(np.tril(np.ones((8, 8), np.float32), -1).reshape(1, 64), (128, 1)),
    }
    nc = bacc.Bacc("TRN2", target_bir_lowering=False, num_devices=1)
    aps, named = {}, {}
    for name, a in arrays.items():
        a = np.ascontiguousarray(a)
        named["in_" + name] = a
        aps[name] = nc.dram_tensor("in_" + name, a.shape, mybir.dt.from_np(a.dtype), kind="ExternalInput").ap()
    aps["wv_quads"] = aps["wv_rows"].rearrange("(g p) n -> g p n", p=128)
    out = nc.dram_tensor("out_x", (2, 128, 512), F32, kind="ExternalOutput").ap()
    program(nc, aps, out)
    r = run_bass_kernel_spmd(nc, [named], core_ids=[0])
    return r.results[0]["out_x"]
```
